# Optimizing a Trainium2 kernel written in Bass

```python
import numpy as np
import jax
import jax.numpy as jnp

def _softmax(x, axis=-1):
    return jax.nn.softmax(x, axis=axis)
def _gelu(x):
    return jax.nn.gelu(x, approximate=True)
def _silu(x):
    return jax.nn.silu(x)
def _sigmoid(x):
    return jax.nn.sigmoid(x)
def _layernorm(x, axis=-1, eps=1e-5):
    m = jnp.mean(x, axis=axis, keepdims=True)
    v = jnp.var(x, axis=axis, keepdims=True)
    return (x - m) / jnp.sqrt(v + eps)
def _scatter_add(tgt, idx, src, axis=0):
    return tgt.at[idx].add(src)
def _segment_sum(src, seg, n):
    return jax.ops.segment_sum(src, seg, n)

kernel_name = 'mk_adj_resnorm_d2_adj_512_d1fbb5'

def setup_inputs(seed: int = 0):
    np.random.seed(seed)
    _w = jnp.asarray
    def _rec_inputs():
        import jax
        import jax.numpy as jnp
        _gk = jax.random.key(seed)
        x = -0.0005207 + 1.001 * jax.random.normal(jax.random.fold_in(_gk, 1), (16, 1024, 512), jnp.float32)
        _a = jax.random.bernoulli(jax.random.fold_in(_gk, 2), 0.015625, (16, 1024, 1024))
        adj = _a.astype(jnp.int32)
        return x, adj
    x, adj = _rec_inputs()
    def _L0_gnn_setup():
        import jax, jax.numpy as jnp
        import numpy as np
        NEG_INF = -1e+30
        NEG_SLOPE = 0.2
        key = jax.random.key(seed)
        k1, k2, k3, k4, k5 = jax.random.split(key, 5)
        B, N, D, H = (2, 2048, 512, 8)
        k = D // H
        return {'x': jax.random.normal(k1, (B, N, D), dtype=jnp.float32), 'A': jax.random.randint(k2, (B, N, N), 0, 2, dtype=jnp.int32), 'W_proj': jax.random.normal(k3, (D, D), dtype=jnp.float32) * (1.0 / np.sqrt(D)), 'W_att': jax.random.normal(k4, (H, 2 * k), dtype=jnp.float32) * (1.0 / np.sqrt(2 * k)), 'b_att': jax.random.normal(k5, (H,), dtype=jnp.float32) * 0.01}
    _L0_gnn_all = _L0_gnn_setup()
    _L0_gnn_in = {k: v for k, v in _L0_gnn_all.items() if k in ('W_proj', 'W_att', 'b_att', )}
    del _L0_gnn_all

    def _L1_gnn_setup():
        import jax, jax.numpy as jnp
        import numpy as np
        NEG_INF = -9000000000000000.0
        ALPHA = 0.2
        key = jax.random.key(seed)
        k1, k2, k3, k4, k5 = jax.random.split(key, 5)
        B, N, F_in, F_out, H = (4, 2048, 512, 64, 8)
        x = jax.random.normal(k1, (B, N, F_in), dtype=jnp.float32)
        adj = jax.random.randint(k2, (B, N, N), 0, 2, dtype=jnp.int32)
        W = jax.random.normal(k3, (H, F_in, F_out), dtype=jnp.float32) * (1.0 / np.sqrt(F_in))
        a1 = jax.random.normal(k4, (H, F_out), dtype=jnp.float32) * (1.0 / np.sqrt(2 * F_out))
        a2 = jax.random.normal(k5, (H, F_out), dtype=jnp.float32) * (1.0 / np.sqrt(2 * F_out))
        return {'x': x, 'adj': adj, 'W': W, 'a1': a1, 'a2': a2}
    _L1_gnn_all = _L1_gnn_setup()
    _L1_gnn_in = {k: v for k, v in _L1_gnn_all.items() if k in ('W', 'a1', 'a2', )}
    del _L1_gnn_all

    return {
        "x": x,
        "adj": adj,
        "L0_gnn_W_proj": _L0_gnn_in["W_proj"],
        "L0_gnn_W_att": _L0_gnn_in["W_att"],
        "L0_gnn_b_att": _L0_gnn_in["b_att"],
        "L1_gnn_W": _L1_gnn_in["W"],
        "L1_gnn_a1": _L1_gnn_in["a1"],
        "L1_gnn_a2": _L1_gnn_in["a2"],
    }

def reference(x, adj, L0_gnn_W_proj, L0_gnn_W_att, L0_gnn_b_att, L1_gnn_W, L1_gnn_a1, L1_gnn_a2):
    import jax
    import jax.numpy as jnp
    def _L0_gnn_ref(x, A, W_proj, W_att, b_att):
        import jax, jax.numpy as jnp
        import numpy as np
        NEG_INF = -1e+30
        NEG_SLOPE = 0.2
        B, N, _ = x.shape
        H, two_k = W_att.shape
        k = two_k // 2
        xp = jnp.einsum('bnd,do->bno', x, W_proj)
        xh = xp.reshape(B, N, H, k).transpose(0, 2, 1, 3)
        a_src = jnp.einsum('bhnk,hk->bhn', xh, W_att[:, :k])
        a_dst = jnp.einsum('bhnk,hk->bhn', xh, W_att[:, k:])
        scores = a_src[:, :, :, None] + a_dst[:, :, None, :] + b_att[None, :, None, None]
        scores = jax.nn.leaky_relu(scores, negative_slope=NEG_SLOPE)
        mask = (A > 0)[:, None, :, :]
        scores = jnp.where(mask, scores, NEG_INF)
        att = jax.nn.softmax(scores, axis=-1)
        out = jax.nn.relu(jnp.einsum('bhij,bhjk->bhik', att, xh))
        return out.transpose(0, 2, 1, 3).reshape(B, N, H * k)

    def _L1_gnn_ref(x, adj, W, a1, a2):
        import jax, jax.numpy as jnp
        import numpy as np
        NEG_INF = -9000000000000000.0
        ALPHA = 0.2
        h = jnp.einsum('bnf,hfo->bhno', x, W)
        s1 = jnp.einsum('bhno,ho->bhn', h, a1)
        s2 = jnp.einsum('bhno,ho->bhn', h, a2)
        e = jax.nn.leaky_relu(s1[..., :, None] + s2[..., None, :], negative_slope=ALPHA)
        mask = (adj > 0)[:, None, :, :]
        attn = jax.nn.softmax(jnp.where(mask, e, NEG_INF), axis=-1)
        h_prime = jnp.einsum('bhnm,bhmo->bhno', attn, h)
        B, H, N, Fo = h_prime.shape
        return jnp.transpose(h_prime, (0, 2, 1, 3)).reshape(B, N, H * Fo)

    x = _layernorm(x + _L0_gnn_ref(x, adj, L0_gnn_W_proj, L0_gnn_W_att, L0_gnn_b_att), axis=-1)
    x = _layernorm(x + _L1_gnn_ref(x, adj, L1_gnn_W, L1_gnn_a1, L1_gnn_a2), axis=-1)
    return x


_drawn_inputs = setup_inputs


def setup_inputs(seed=0):
    import zlib

    import numpy as np

    out = dict(_drawn_inputs(seed))
    spreads = {}
    factors = {'L0_gnn_b_att': 64.0}
    for name, (base, spread) in spreads.items():
        noise = np.random.default_rng([zlib.crc32(name.encode()), seed]).standard_normal(out[name].shape)
        drawn = base * np.exp(spread * noise) if base else spread * noise
        out[name] = jnp.asarray(drawn.astype(out[name].dtype))
    for name, factor in factors.items():
        out[name] = (out[name] * factor).astype(out[name].dtype)
    return out
```

```python
import numpy as np

import concourse.bass as bass
from concourse import mybir
from contextlib import ExitStack

fp32 = mybir.dt.float32
bf16 = mybir.dt.bfloat16
fp8 = mybir.dt.float8e4
int32 = mybir.dt.int32
ALU = mybir.AluOpType
ACT = mybir.ActivationFunctionType
AX = mybir.AxisListType

P = 128
B, N, D = 16, 1024, 512
H, K = 8, 64
T = N // P
F = D // P
KD = K + 1
PARTS = 3
W3 = PARTS * KD
UNITS = 2 * B
SLOPE = 0.2
EPS = 1e-5
EDGE = 2.0 ** -6
SIGN_TO_EDGE = 4
CHUNK = 2
NCHUNK = T // CHUNK
HALF = T // 2
assert H * K == D


def gat_two_layers(nc, x, adj, W0, att0, b0, W1, a1, a2, ident_in, select_in, out):
    ctx = ExitStack()
    with ctx:
        def sb(name, shape, dt):
            return ctx.enter_context(nc.sbuf_tensor(name, shape, dt))

        def pb(name, shape, dt):
            return ctx.enter_context(nc.psum_tensor(name, shape, dt))

        def sem(name):
            return ctx.enter_context(nc.semaphore(name))

        ident = sb("ident", [P, P], fp32)
        ident_b = sb("ident_b", [P, P], bf16)
        ones = sb("ones", [P, P], fp32)
        select = sb("select", [P, H, P], bf16)
        weight = [sb(f"weight{l}", [P, F, D], fp32) for l in range(2)]
        score_w = [sb(f"score_w{l}", [P, F, 2 * H], fp32) for l in range(2)]
        score_b = sb("score_b", [P, 2, 2 * H], fp32)
        half_neg = sb("half_neg", [P, HALF], fp32)
        xs = [sb(f"xs{p}", [P, T, D], fp32) for p in range(2)]
        mask = [sb(f"mask{p}", [P, T, N], fp8) for p in range(2)]
        adj_rows = sb("adj_rows", [P, 2, N], bf16)
        xT = sb("xT", [P, 2, F, P], fp32)
        h_ones = [sb(f"h_ones{q}", [P, T, H, KD], fp32) for q in range(2)]
        sd = [sb(f"sd{q}", [P, T, 2 * H], fp32) for q in range(2)]
        sT = [sb(f"sT{q}", [P, N], bf16) for q in range(2)]
        s_parts = sb("s_parts", [P, T, P], bf16)
        s_rest = sb("s_rest", [P, T, H], fp32)
        d_max = sb("d_max", [P, P], fp32)
        d_maxT = sb("d_maxT", [P, 1], fp32)
        d_diag = sb("d_diag", [P, H], fp32)
        d_top = sb("d_top", [P, H], fp32)
        zt = sb("zt", [P, T, H], fp32)
        args = sb("args", [P, 4, T, H], fp32)
        uvpq = [sb(f"uvpq{q}", [P, 4, T, H], fp32) for q in range(2)]
        h_sum = sb("h_sum", [P, D], fp32)
        h_mean = [sb(f"h_mean{q}", [P, H, K], fp32) for q in range(2)]
        neg = [sb(f"neg{k}", [P, T, N], fp8) for k in range(2)]
        pos = [sb(f"pos{k}", [P, T, N], fp8) for k in range(2)]
        y = sb("y", [P, 2, T, KD], fp32)
        y_parts = [sb(f"y_parts{k}", [P, 2, T, PARTS, KD], bf16) for k in range(2)]
        sums = [sb(f"sums{k}", [P, T, 2, KD], fp32) for k in range(2)]
        den = [sb(f"den{k}", [P, 3, T], fp32) for k in range(2)]
        o = sb("o", [P, T, D], fp32)
        stats = sb("stats", [P, T, 6], fp32)
        mv = sb("mv", [P, T, 2], fp32)
        rstd = sb("rstd", [P, T], fp32)
        staged = sb("staged", [P, 2, 2, D], fp32)

        s_ps = [pb(f"s_ps{k}", [P, N], fp32) for k in range(2)]
        acc = [pb(f"acc{k}", [P, 512], fp32) for k in range(2)]
        misc = pb("misc", [P, 512], fp32)
        misc_b = misc[:, :].bitcast(bf16).rearrange("p (t n) -> p t n", t=T)
        wide = pb("wide", [P, 512], fp32)

        const_in = sem("const_in")
        w_in = sem("w_in")
        att_in = sem("att_in")
        x_in = [[sem(f"x_in{p}{k}") for k in range(2)] for p in range(2)]
        adj_in = [sem(f"adj_in{k}") for k in range(2)]
        out_stored = [sem(f"out_stored{k}") for k in range(2)]
        setup_dve = sem("setup_dve")
        setup_pool = sem("setup_pool")
        passed = sem("passed")
        s_rows = sem("s_rows")
        attended = sem("attended")
        xT_ps = sem("xT_ps")
        h_ps = sem("h_ps")
        sd_ps = sem("sd_ps")
        mask_ps = sem("mask_ps")
        guard_ps = sem("guard_ps")
        sT_ps = sem("sT_ps")
        mean_ps = sem("mean_ps")
        signed = sem("signed")
        xT_copied = sem("xT_copied")
        h_copied = sem("h_copied")
        exps = sem("exps")
        mean_copied = sem("mean_copied")
        rounded = sem("rounded")
        acc_read = sem("acc_read")
        neg_made = sem("neg_made")
        edges = sem("edges")
        rest = sem("rest")
        sd_copied = sem("sd_copied")
        mask_copied = sem("mask_copied")
        guard = sem("guard")
        sT_made = sem("sT_made")
        sT_copied = sem("sT_copied")
        dens = sem("dens")
        residual = sem("residual")
        normed = sem("normed")
        applied = sem("applied")
        scaled = sem("scaled")
        combined = sem("combined")
        summed = sem("summed")
        rstds = sem("rstds")

        GUARD = 6

        def wait(eng, s, value):
            if not isinstance(value, int) or value > 0:
                eng.wait_ge(s, value)

        def stand_apart(eng):
            eng.sem_inc(passed, 1)

        def phases(eng, phase):
            phase(-1, 3)
            phase(0, 0)
            loops = B // 2 - 1
            with eng.Fori(0, loops) as i:
                for phi in (1, 2, 3):
                    phase(i, phi)
                phase(i + 1, 0)
            for phi in (1, 2, 3):
                phase(loops, phi)
            phase(loops + 1, 0)

        def parts_of(pair, phi):
            if not isinstance(pair, int):
                return True, True, True
            u = 4 * pair + phi
            return 0 <= u < UNITS, u + 1 < UNITS, u - 1 >= 0

        def next_phase(pair, phi):
            return (pair, phi + 1) if phi < 3 else (pair + 1, 0)

        def prev_phase(pair, phi):
            return (pair, phi - 1) if phi > 0 else (pair - 1, 3)

        def graph_of(pair, phi):
            return 2 * pair + phi % 2

        def mask_graph(pair, phi):
            return graph_of(*next_phase(pair, phi)) if phi in (0, 3) else None

        mask_jobs = {0: (2, 5), 1: (2, 5), 2: (0,), 3: (0,), 4: (0,), 5: (0,)}
        prep_heads = (2, 3, 4, 5)

        def mask_tile(h, it):
            at = [(a, b) for a in sorted(mask_jobs) for b in mask_jobs[a]]
            return at.index((h, it)) if (h, it) in at else None

        def heads_ahead(pair, phi, h):
            attn, prep, _ = parts_of(pair, phi)
            if h < H - 1:
                return (pair, phi, h + 1) if attn else None
            return (*next_phase(pair, phi), 0) if prep else None

        def head_behind(pair, phi, h):
            attn, _, ends = parts_of(pair, phi)
            if h > 0:
                return (pair, phi, h - 1) if attn else None
            return (*prev_phase(pair, phi), H - 1) if ends else None

        def unit(pair, phi):
            return 4 * pair + phi

        block = ctx.enter_context(nc.Block())

        @block.sync
        def _(sp):
            sp.dma_start(ident[:, :], ident_in).then_inc(const_in, 16)
            sp.dma_start(select[:, :, :].bitcast(mybir.dt.uint16), select_in).then_inc(const_in, 16)
            sp.dma_start(weight[0][:, :, :], W0.rearrange("(k p) o -> p k o", p=P)).then_inc(w_in, 16)
            for k in range(F):
                sp.dma_start(weight[1][:, k, :].rearrange("p (h o) -> p h o", h=H),
                             W1[:, k * P:(k + 1) * P, :].rearrange("h p o -> p h o")).then_inc(w_in, 16)
            for n, v in enumerate((att0[:, 0:K], att0[:, K:2 * K], a1, a2)):
                sp.dma_start(o[:, n, :].rearrange("p (h o) -> p h o", h=H),
                             v.rearrange("(a h) o -> a h o", a=1).to_broadcast([P, H, K])).then_inc(att_in, 16)
            sp.dma_start(score_b[:, 0, 0:H], b0.rearrange("(a h) -> a h", a=1).to_broadcast([P, H]))\
              .then_inc(att_in, 16)

            def load_x(g, p, half):
                tiles = slice(half * HALF, (half + 1) * HALF)
                src = x[bass.ds(g, 1)].rearrange("a (t p) d -> p (a t) d", p=P)
                sp.dma_start(xs[p][:, tiles, :], src[:, tiles, :]).then_inc(x_in[p][half], 16)

            for half in range(2):
                load_x(0, 0, half)

            def phase(pair, phi):
                attn, prep, ends = parts_of(pair, phi)
                done = T * unit(*prev_phase(pair, phi))
                g = graph_of(*prev_phase(pair, phi))
                final = ends and phi in (0, 3)
                for k in range(T // 2):
                    if final:
                        wait(sp, applied, done + 2 * (k + 1))
                        dst = out[bass.ds(g, 1)].rearrange("a (t p) d -> p (a t) d", p=P)
                        sp.dma_start(dst[:, 2 * k:2 * k + 2, :], staged[:, k % 2, :, :])\
                          .then_inc(out_stored[k % 2], 16)
                    if k % 2 == 1 and prep and attn and phi in (0, 3):
                        load_x(mask_graph(pair, phi), (phi + 1) % 2, k // 2)

            phases(sp, phase)
            for k in range(2):
                sp.wait_ge(out_stored[k], 16 * (2 * B + 1))

        @block.gpsimd
        def _(pool):
            def load_adj(g, it):
                src = adj[bass.ds(g, 1)].rearrange("a (t p) j -> p (a t) j", p=P)
                pool.dma_start(adj_rows[:, it % 2, :], src[:, it, :]).then_inc(adj_in[it % 2], 16)

            nc.gpsimd.memset(half_neg[:, :], -0.5).then_inc(setup_pool, 1)
            nc.gpsimd.memset(h_ones[0][:, :, :, K:KD], 1.0).then_inc(setup_pool, 1)
            nc.gpsimd.memset(h_ones[1][:, :, :, K:KD], 1.0).then_inc(setup_pool, 1)
            pool.wait_ge(setup_pool, 3)
            load_adj(0, 0)
            load_adj(0, 1)

            def scale_head(pair, phi, h):
                u, q = unit(pair, phi), phi % 2
                g = H * u + h
                if h == 0:
                    pool.wait_ge(exps, u + 1)
                    pool.wait_ge(h_copied, T * (u + 1))
                for k in range(2):
                    wait(pool, rest, 4 * g - 1 + k)
                    factor = uvpq[q][:, 2 + k, :, h:h + 1].to_broadcast([P, T, KD])
                    nc.gpsimd.tensor_tensor(y[:, k], h_ones[q][:, :, h, :], factor, ALU.mult).then_inc(scaled, 1)

            def combine_head(pair, phi, h):
                u, q = unit(pair, phi), phi % 2
                g = H * u + h
                s, r = sums[h % 2], den[h % 2]
                pool.wait_ge(acc_read, T * (g + 1))
                for k in range(2):
                    factor = uvpq[q][:, k, :, h:h + 1].to_broadcast([P, T, KD])
                    nc.gpsimd.tensor_tensor(s[:, :, k, :], s[:, :, k, :], factor, ALU.mult).then_inc(combined, 1)
                pool.wait_ge(combined, 6 * g + 2)
                nc.gpsimd.tensor_tensor(s[:, :, 0, :], s[:, :, 0, :], s[:, :, 1, :], ALU.add).then_inc(combined, 1)
                oh, fill = o[:, :, h * K:(h + 1) * K], s[:, :, 1, 0:K]
                pool.wait_ge(dens, 3 * g + 3)
                if h == 0:
                    wait(pool, residual, T * u)
                    pool.wait_ge(mean_copied, u + 1)
                nc.gpsimd.tensor_tensor(fill, r[:, 0:1, :].rearrange("p a t -> p t a").to_broadcast([P, T, K]),
                                        h_mean[q][:, h:h + 1, :].to_broadcast([P, T, K]), ALU.mult)\
                  .then_inc(combined, 1)
                nc.gpsimd.tensor_tensor(oh, s[:, :, 0, 0:K],
                                        r[:, 2:3, :].rearrange("p a t -> p t a").to_broadcast([P, T, K]), ALU.mult)\
                  .then_inc(combined, 1)
                pool.wait_ge(combined, 6 * g + 5)
                nc.gpsimd.tensor_tensor(oh, oh, fill, ALU.add).then_inc(combined, 1)

            def rstd_half(pair, phi, half):
                u = unit(pair, phi)
                tiles = slice(half * HALF, (half + 1) * HALF)
                pool.wait_ge(normed, 2 * (T * u + HALF * (half + 1)))
                stand_apart(pool)
                nc.gpsimd.tensor_scalar(rstd[:, tiles], mv[:, tiles, 1], EPS, None, ALU.add).then_inc(rstds, 1)
                pool.wait_ge(rstds, 4 * u + 2 * half + 1)
                nc.gpsimd.tensor_tensor(rstd[:, tiles], rstd[:, tiles], half_neg[:, :], ALU.pow).then_inc(rstds, 1)

            def sum_tile(pair, phi, t):
                u, q = unit(pair, phi), phi % 2
                if t == 0:
                    return
                pool.wait_ge(h_copied, T * u + t + 1)
                if t == 1:
                    wait(pool, mean_ps, u)
                else:
                    pool.wait_ge(summed, (T - 1) * u + t - 1)
                first = h_ones[q][:, 0, :, 0:K] if t == 1 else h_sum[:, :].rearrange("p (h o) -> p h o", h=H)
                nc.gpsimd.tensor_tensor(h_sum[:, :].rearrange("p (h o) -> p h o", h=H), first,
                                        h_ones[q][:, t, :, 0:K], ALU.add).then_inc(summed, 1)

            def phase(pair, phi):
                attn, prep, ends = parts_of(pair, phi)
                if phi == 1 and not (isinstance(pair, int) and pair == B // 2 - 1):
                    pool.wait_ge(mask_ps, T * (2 * pair + 2))
                    for it in range(2):
                        load_adj(2 * pair + 2, it)
                for h in range(H):
                    ahead, behind = heads_ahead(pair, phi, h), head_behind(pair, phi, h)
                    if ahead:
                        scale_head(*ahead)
                    if behind:
                        combine_head(*behind)
                    if ends and h in (1, 2):
                        rstd_half(*prev_phase(pair, phi), h - 1)
                    if prep and h in prep_heads:
                        for k in range(2):
                            sum_tile(*next_phase(pair, phi), 2 * (h - prep_heads[0]) + k)
                    if prep and phi in (0, 3):
                        g = mask_graph(pair, phi)
                        for it in mask_jobs.get(h, ()):
                            t = mask_tile(h, it)
                            if t < T - 2 or phi == 3:
                                pool.wait_ge(mask_ps, T * g + t + 1)
                                load_adj(g if t < T - 2 else g + 1, (t + 2) % T)

            phases(pool, phase)

        @block.scalar
        def _(act):
            def sign_tile(pair, phi, h, t):
                u, q = unit(pair, phi), phi % 2
                g = H * u + h
                if t == 0:
                    act.wait_ge(s_rows, g + 1)
                    act.wait_ge(sd_copied, T * (u + 1))
                    wait(act, attended, T * (g - 1))
                    stand_apart(act)
                nc.scalar.activation(neg[h % 2][:, t, :], s_ps[h % 2][:, :], ACT.Sign,
                                     bias=sd[q][:, t, H + h:H + h + 1], saturate=False).then_inc(signed, 1)

            def round_part(pair, phi, h, part, k):
                g = H * unit(pair, phi) + h
                if part == 0:
                    act.wait_ge(scaled, 2 * g + k + 1)
                else:
                    act.wait_ge(rest, 4 * g + k + 1)
                nc.scalar.activation(y_parts[h % 2][:, k, :, part, :], y[:, k], ACT.Copy).then_inc(rounded, 1)

            def copy_xT(pair, phi, t):
                n = T * unit(pair, phi) + t
                act.wait_ge(xT_ps, n + 1)
                wait(act, sd_ps, n - 1)
                nc.scalar.activation(xT[:, t % 2], misc[:, :].rearrange("p (k n) -> p k n", k=F), ACT.Copy)\
                  .then_inc(xT_copied, 1)

            def copy_h(pair, phi, t):
                act.wait_ge(h_ps, T * unit(pair, phi) + t + 1)
                nc.scalar.activation(h_ones[phi % 2][:, t, :, 0:K], wide[:, :].rearrange("p (h o) -> p h o", h=H),
                                     ACT.Copy).then_inc(h_copied, 1)

            def phase(pair, phi):
                _, prep, _ = parts_of(pair, phi)
                nxt = next_phase(pair, phi)
                for h in range(H):
                    ahead = heads_ahead(pair, phi, h)
                    for t in range(T):
                        if h == 6 and t == 6 and prep:
                            act.wait_ge(guard, GUARD * (unit(*nxt) + 1))
                            nc.scalar.activation(uvpq[nxt[1] % 2][:, :, :, :], args[:, :, :, :], ACT.Exp)\
                              .then_inc(exps, 1)
                        if ahead:
                            sign_tile(*ahead, t)
                            if t in (1, 2, 4, 6):
                                round_part(*ahead, *{1: (0, 0), 2: (0, 1), 4: (1, 0), 6: (1, 1)}[t])
                        if prep and h in prep_heads and t in (1, 3, 5, 7):
                            tile = 2 * (h - prep_heads[0]) + t // 4
                            (copy_xT if t in (1, 5) else copy_h)(*nxt, tile)
                    if h == 7 and prep:
                        act.wait_ge(mean_ps, unit(*nxt) + 1)
                        nc.scalar.activation(h_mean[nxt[1] % 2][:, :, :],
                                             wide[:, :].rearrange("p (h o) -> p h o", h=H), ACT.Copy,
                                             scale=1.0 / N).then_inc(mean_copied, 1)

            act.wait_ge(setup_pool, 3)
            phases(act, phase)

        @block.vector
        def _(dve):
            chain = [0]

            def link(ins):
                chain[0] += 1
                ins.then_inc(setup_dve, 1)
                dve.wait_ge(setup_dve, chain[0])

            nc.vector.memset(ones[:, :], 1.0)
            for k in range(2):
                nc.vector.memset(staged[:, k, :, :], 0.0).then_inc(out_stored[k], 16)
            nc.vector.memset(d_max[:, :], 0.0)
            nc.vector.memset(s_parts[:, :, :], 0.0)
            link(nc.vector.memset(score_b[:, 1, :], 0.0))
            link(nc.vector.memset(score_b[:, 0, H:2 * H], 0.0))
            dve.wait_ge(const_in, 32)
            link(nc.vector.tensor_copy(ident_b[:, :], ident[:, :]))
            dve.wait_ge(w_in, 16 * (1 + F))
            dve.wait_ge(att_in, 16 * 5)
            for l in range(2):
                for n in range(2):
                    vec = o[:, 2 * l + n, :].rearrange("p (a c) -> p a c", a=1).to_broadcast([P, F, D])
                    tmp = o[:, 4:4 + F, :]
                    link(nc.vector.tensor_tensor(tmp, weight[l][:, :, :], vec, ALU.mult))
                    link(nc.vector.tensor_reduce(score_w[l][:, :, n * H:(n + 1) * H],
                                                 tmp.rearrange("p k (h o) -> p k h o", h=H), AX.X, ALU.add))

            def read_acc(pair, phi, h, it):
                g = H * unit(pair, phi) + h
                dve.wait_ge(attended, T * g + it + 1)
                if it == 0:
                    wait(dve, combined, 6 * (g - 1))
                nc.vector.tensor_reduce(sums[h % 2][:, it],
                                        acc[it % 2][:, 0:2 * W3].rearrange("p (k s c) -> p k c s", k=2, s=PARTS),
                                        AX.X, ALU.add).then_inc(acc_read, 1)

            def make_edges(pair, phi, h, c):
                g = H * unit(pair, phi) + h
                tiles = slice(c * CHUNK, (c + 1) * CHUNK)
                n32, p32, m32 = (b[:, tiles, :].bitcast(int32) for b in (neg[h % 2], pos[h % 2], mask[phi % 2]))
                dve.wait_ge(signed, T * g + CHUNK * (c + 1))
                nc.vector.scalar_tensor_tensor(n32, n32, SIGN_TO_EDGE, m32, ALU.logical_shift_right,
                                               ALU.bitwise_and).then_inc(neg_made, 1)
                dve.wait_ge(neg_made, NCHUNK * g + c + 1)
                nc.vector.tensor_tensor(p32, n32, m32, ALU.bitwise_xor).then_inc(edges, 1)

            def split_y(pair, phi, h, part, k):
                g = H * unit(pair, phi) + h
                yp = y_parts[h % 2]
                dve.wait_ge(rounded, 4 * g + 2 * part + k + 1)
                dst = y[:, k] if part == 0 else yp[:, k, :, 2, :]
                nc.vector.tensor_tensor(dst, y[:, k], yp[:, k, :, part, :], ALU.subtract).then_inc(rest, 1)

            def denominators(pair, phi, h):
                g = H * unit(pair, phi) + h
                s, r = sums[h % 2], den[h % 2]
                dve.wait_ge(combined, 6 * g + 3)
                nc.vector.tensor_scalar(r[:, 0, :], s[:, :, 0, K], 0.0, None, ALU.is_equal).then_inc(dens, 1)
                dve.wait_ge(dens, 3 * g + 1)
                nc.vector.tensor_tensor(r[:, 1, :], s[:, :, 0, K], r[:, 0, :], ALU.add).then_inc(dens, 1)
                dve.wait_ge(dens, 3 * g + 2)
                nc.vector.reciprocal(r[:, 2, :], r[:, 1, :]).then_inc(dens, 1)

            def add_residual(pair, phi, t):
                u, p = unit(pair, phi), phi % 2
                if t == 0:
                    dve.wait_ge(combined, 6 * H * (u + 1))
                if phi < 2:
                    nc.vector.scalar_tensor_tensor(xs[p][:, t, :], o[:, t, :], 0.0, xs[p][:, t, :], ALU.max, ALU.add)\
                      .then_inc(residual, 1)
                else:
                    nc.vector.tensor_tensor(xs[p][:, t, :], o[:, t, :], xs[p][:, t, :], ALU.add).then_inc(residual, 1)

            def norm_tile(pair, phi, t):
                n = T * unit(pair, phi) + t
                dve.wait_ge(residual, n + 1)
                nc.vector.bn_stats(stats[:, t, :], xs[phi % 2][:, t, :]).then_inc(normed, 1)
                dve.wait_ge(normed, 2 * n + 1)
                stand_apart(dve)
                nc.vector.bn_aggr(mv[:, t, :], stats[:, t, :]).then_inc(normed, 1)

            def apply_tile(pair, phi, t):
                u, p = unit(pair, phi), phi % 2
                dst = xs[p][:, t, :] if phi < 2 else staged[:, t // 2 % 2, t % 2, :]
                if t % HALF == 0:
                    dve.wait_ge(rstds, 4 * u + 2 * (t // HALF + 1))
                if phi >= 2 and t % 2 == 0:
                    wait(dve, out_stored[t // 2 % 2], 16 * (2 * graph_of(pair, phi) + t // 4 + 1))
                nc.vector.tensor_scalar(dst, xs[p][:, t, :], mv[:, t, 0:1], rstd[:, t:t + 1], ALU.subtract, ALU.mult)\
                  .then_inc(applied, 1)

            def copy_sd(pair, phi, t):
                u = unit(pair, phi)
                dve.wait_ge(sd_ps, T * u + t + 1)
                nc.vector.tensor_tensor(sd[phi % 2][:, t, :], misc[:, 0:2 * H], score_b[:, phi // 2, :], ALU.add)\
                  .then_inc(sd_copied, 1)

            def copy_mask(g, p, it):
                dve.wait_ge(mask_ps, T * g + it + 1)
                stand_apart(dve)
                nc.vector.tensor_scalar(mask[p][:, :, it * P:(it + 1) * P], misc_b, 0.0, EDGE, ALU.is_gt, ALU.mult, saturate=False)\
                  .then_inc(mask_copied, 1)

            def guard_a(pair, phi):
                u, q = unit(pair, phi), phi % 2
                s, d = sd[q][:, :, 0:H], sd[q][:, :, H:2 * H]
                dve.wait_ge(sd_copied, T * (u + 1))
                nc.vector.tensor_reduce(d_max[:, 0:H], d.rearrange("p t h -> p h t"), AX.X, ALU.max)\
                  .then_inc(guard, 1)
                nc.vector.tensor_copy(s_parts[:, :, 0:H], s).then_inc(sT_made, 1)
                dve.wait_ge(sT_made, 4 * u + 1)
                nc.vector.tensor_tensor(s_rest[:, :, :], s, s_parts[:, :, 0:H], ALU.subtract).then_inc(sT_made, 1)
                dve.wait_ge(sT_made, 4 * u + 2)
                nc.vector.tensor_copy(s_parts[:, :, H:2 * H], s_rest[:, :, :]).then_inc(sT_made, 1)
                dve.wait_ge(sT_made, 4 * u + 3)
                nc.vector.tensor_tensor(s_parts[:, :, 2 * H:3 * H], s_rest[:, :, :], s_parts[:, :, H:2 * H],
                                        ALU.subtract).then_inc(sT_made, 1)

            def guard_b(pair, phi):
                u = unit(pair, phi)
                dve.wait_ge(guard_ps, 2 * u + 1)
                nc.vector.tensor_reduce(d_maxT[:, :], misc[:, 0:P], AX.X, ALU.max).then_inc(guard, 1)
                dve.wait_ge(guard, GUARD * u + 2)
                nc.vector.tensor_scalar(d_diag[:, :], ident[:, 0:H], d_maxT[:, 0:1], None, ALU.mult)\
                  .then_inc(guard, 1)

            def guard_c(pair, phi):
                u, q = unit(pair, phi), phi % 2
                s, d = sd[q][:, :, 0:H], sd[q][:, :, H:2 * H]
                dve.wait_ge(guard_ps, 2 * u + 2)
                nc.vector.tensor_copy(d_top[:, :], misc[:, 0:H]).then_inc(guard, 1)
                dve.wait_ge(guard, GUARD * u + 4)
                top = d_top[:, :].rearrange("p (a h) -> p a h", a=1).to_broadcast([P, T, H])
                nc.vector.tensor_tensor(args[:, 2], d, top, ALU.subtract)
                nc.vector.tensor_tensor(zt[:, :, :], s, top, ALU.add).then_inc(guard, 1)
                dve.wait_ge(guard, GUARD * u + 5)
                nc.vector.tensor_scalar(args[:, 0], zt[:, :, :], 1.0 - SLOPE, 0.0, ALU.mult, ALU.min)
                nc.vector.tensor_scalar(args[:, 1], zt[:, :, :], SLOPE - 1.0, 0.0, ALU.mult, ALU.min)
                nc.vector.tensor_scalar(args[:, 3], args[:, 2], SLOPE, None, ALU.mult).then_inc(guard, 1)

            def copy_sT(pair, phi):
                dve.wait_ge(sT_ps, unit(pair, phi) + 1)
                nc.vector.tensor_copy(sT[phi % 2][:, :].rearrange("p (t n) -> p t n", t=T), misc_b)\
                  .then_inc(sT_copied, 1)

            def phase(pair, phi):
                attn, prep, ends = parts_of(pair, phi)
                nxt, prv = next_phase(pair, phi), prev_phase(pair, phi)
                for h in range(H):
                    ahead, behind = heads_ahead(pair, phi, h), head_behind(pair, phi, h)
                    for it in range(T):
                        if attn:
                            read_acc(pair, phi, h, it)
                        if prep and phi in (0, 3) and mask_tile(h, it) is not None:
                            copy_mask(mask_graph(pair, phi), (phi + 1) % 2, mask_tile(h, it))
                        if ahead and it in (2, 3, 5, 7):
                            split_y(*ahead, *{2: (0, 0), 3: (0, 1), 5: (1, 0), 7: (1, 1)}[it])
                        if ahead and it % 2 == 1:
                            make_edges(*ahead, it // 2)
                        if behind and it == 6:
                            denominators(*behind)
                        if ends:
                            if h == 1 and it < HALF:
                                for k in range(2):
                                    add_residual(*prv, 2 * it + k)
                            if h == 1 and it >= HALF:
                                norm_tile(*prv, it - HALF)
                            if h == 2 and it < HALF:
                                norm_tile(*prv, it + HALF)
                            if h in (2, 3) and it in (0, 1):
                                for k in range(2):
                                    apply_tile(*prv, HALF * (h - 2) + 2 * it + k)
                        if prep and h in prep_heads and it in (3, 7):
                            copy_sd(*nxt, 2 * (h - prep_heads[0]) + it // 4)
                        if prep and h == 6:
                            if it == 0:
                                guard_a(*nxt)
                            if it == 2:
                                guard_b(*nxt)
                            if it == 4:
                                guard_c(*nxt)
                            if it == 6:
                                copy_sT(*nxt)

            phases(dve, phase)

        @block.tensor
        def _(pe):
            def rows_of_s(pair, phi, h):
                u, q = unit(pair, phi), phi % 2
                g = H * u + h
                if h == 0:
                    pe.wait_ge(sT_copied, u + 1)
                wait(pe, signed, T * (g - 1))
                for k in range(2):
                    last = nc.tensor.matmul(s_ps[h % 2][:, k * 512:(k + 1) * 512], select[:, h, :],
                                            sT[q][:, k * 512:(k + 1) * 512], start=True, stop=True)
                last.then_inc(s_rows, 1)

            def attend(pair, phi, h, it):
                g = H * unit(pair, phi) + h
                n = T * g + it
                wait(pe, acc_read, n - 1)
                if it == 0:
                    pe.wait_ge(rest, 4 * g + 4)
                stand_apart(pe)
                cols = slice(it * P, (it + 1) * P)
                for k, edge in enumerate((pos[h % 2], neg[h % 2])):
                    for t in range(T):
                        if it == 0 and k == 0 and t % CHUNK == 0:
                            pe.wait_ge(edges, NCHUNK * g + t // CHUNK + 1)
                            stand_apart(pe)
                        last = nc.tensor.matmul(acc[it % 2][:, k * W3:(k + 1) * W3], edge[:, t, cols],
                                                y_parts[h % 2][:, k, t].rearrange("p s c -> p (s c)"),
                                                start=(t == 0), stop=(t == T - 1))
                last.then_inc(attended, 1)

            def transpose_mask(g, it):
                pe.wait_ge(adj_in[it % 2], 16 * (T // 2 * g + it // 2 + 1))
                for t in range(T):
                    last = nc.tensor.transpose(misc_b[:, t, :], adj_rows[:, it % 2, t * P:(t + 1) * P], ident_b[:, :])
                last.then_inc(mask_ps, 1)

            def transpose_x(pair, phi, t):
                u, p = unit(pair, phi), phi % 2
                if phi < 2:
                    if t % HALF == 0:
                        pe.wait_ge(x_in[p][t // HALF], 16 * (pair + 1))
                else:
                    pe.wait_ge(applied, T * (u - 2) + t + 1)
                for k in range(F):
                    last = nc.tensor.transpose(misc[:, k * P:(k + 1) * P], xs[p][:, t, k * P:(k + 1) * P], ident[:, :])
                last.then_inc(xT_ps, 1)

            def project(pair, phi, t):
                u, l = unit(pair, phi), phi // 2
                n = T * u + t
                pe.wait_ge(xT_copied, n + 1)
                if t == 0:
                    wait(pe, mean_copied, u)
                else:
                    pe.wait_ge(h_copied, n)
                for k in range(F):
                    last = nc.tensor.matmul(wide[:, :], xT[:, t % 2, k, :], weight[l][:, k, :],
                                            start=(k == 0), stop=(k == F - 1))
                last.then_inc(h_ps, 1)
                for k in range(F):
                    last = nc.tensor.matmul(misc[:, 0:2 * H], xT[:, t % 2, k, :], score_w[l][:, k, :],
                                            start=(k == 0), stop=(k == F - 1))
                last.then_inc(sd_ps, 1)

            def phase(pair, phi):
                attn, prep, ends = parts_of(pair, phi)
                nxt = next_phase(pair, phi)
                u = unit(*nxt)
                empty = (sT_copied, u)
                for h in range(H):
                    ahead = heads_ahead(pair, phi, h)
                    if ahead and attn:
                        rows_of_s(*ahead)
                    for it in range(T):
                        if attn:
                            attend(pair, phi, h, it)
                        if not prep:
                            continue
                        if phi in (0, 3) and mask_tile(h, it) is not None:
                            wait(pe, *empty)
                            g, mt = mask_graph(pair, phi), mask_tile(h, it)
                            transpose_mask(g, mt)
                            empty = (mask_copied, T * g + mt + 1)
                        if h in prep_heads and it in (1, 3, 4, 6):
                            t = 2 * (h - prep_heads[0]) + it // 4
                            if it in (1, 4):
                                wait(pe, *empty)
                                transpose_x(*nxt, t)
                            else:
                                project(*nxt, t)
                                empty = (sd_copied, T * u + t + 1)
                        if h == 6 and it == 1:
                            wait(pe, *empty)
                            pe.wait_ge(guard, GUARD * u + 1)
                            nc.tensor.transpose(misc[:, 0:P], d_max[:, :], ident[:, :]).then_inc(guard_ps, 1)
                        if h == 6 and it == 3:
                            pe.wait_ge(guard, GUARD * u + 3)
                            nc.tensor.matmul(misc[:, 0:H], ones[:, :], d_diag[:, :], start=True, stop=True)\
                              .then_inc(guard_ps, 1)
                        if h == 6 and it == 5:
                            pe.wait_ge(guard, GUARD * u + 4)
                            pe.wait_ge(sT_made, 4 * (u + 1))
                            for t in range(T):
                                last = nc.tensor.transpose(misc_b[:, t, :], s_parts[:, t, :], ident_b[:, :])
                            last.then_inc(sT_ps, 1)
                        if h == 7 and it == 3:
                            pe.wait_ge(summed, (T - 1) * (u + 1))
                            pe.wait_ge(h_copied, T * (u + 1))
                            nc.tensor.matmul(wide[:, :], ones[:, :], h_sum[:, :], start=True, stop=True)\
                              .then_inc(mean_ps, 1)
                    if ahead and not attn:
                        rows_of_s(*ahead)

            pe.wait_ge(setup_dve, 3 + 8)
            phases(pe, phase)


def kernel(x, adj, L0_gnn_W_proj, L0_gnn_W_att, L0_gnn_b_att, L1_gnn_W, L1_gnn_a1, L1_gnn_a2):
    import concourse.bacc as bacc
    from concourse.bass_utils import run_bass_kernel_spmd

    nc = bacc.Bacc("TRN2", target_bir_lowering=False, num_devices=1)
    select = np.zeros((P, H, P), np.uint16)
    for part in range(PARTS):
        for h in range(H):
            select[part * H + h, h, :] = 0x3F80
    ins = {
        "x": np.ascontiguousarray(x), "adj": np.ascontiguousarray(adj), "W0": np.ascontiguousarray(L0_gnn_W_proj),
        "att0": np.ascontiguousarray(L0_gnn_W_att), "b0": np.ascontiguousarray(L0_gnn_b_att),
        "W1": np.ascontiguousarray(L1_gnn_W), "a1": np.ascontiguousarray(L1_gnn_a1),
        "a2": np.ascontiguousarray(L1_gnn_a2), "ident": np.eye(P, dtype=np.float32), "select": select,
    }
    aps = [nc.dram_tensor(f"in_{n}", a.shape, mybir.dt.from_np(a.dtype), kind="ExternalInput").ap()
           for n, a in ins.items()]
    out = nc.dram_tensor("out_x", (B, N, D), fp32, kind="ExternalOutput").ap()
    gat_two_layers(nc, *aps, out)
    r = run_bass_kernel_spmd(nc, [{f"in_{n}": a for n, a in ins.items()}], core_ids=[0])
    return r.results[0]["out_x"]
```

```python
import numpy as np

import concourse.bass as bass
from concourse import mybir
from contextlib import ExitStack

fp32 = mybir.dt.float32
bf16 = mybir.dt.bfloat16
fp8 = mybir.dt.float8e4
int32 = mybir.dt.int32
ALU = mybir.AluOpType
ACT = mybir.ActivationFunctionType
AX = mybir.AxisListType

P = 128
B, N, D = 16, 1024, 512
H, K = 8, 64
T = N // P
F = D // P
KD = K + 1
PARTS = 3
W3 = PARTS * KD
UNITS = 2 * B
SLOPE = 0.2
EPS = 1e-5
EDGE = 2.0 ** -6
SIGN_TO_EDGE = 4
CHUNK = 2
NCHUNK = T // CHUNK
PAIR = 2
PAIRS = T // PAIR
ACCS = 4
assert H * K == D


def gat_two_layers(nc, x, adj, W0, att0, b0, W1, a1, a2, ident_in, select_in, out):
    ctx = ExitStack()
    with ctx:
        def sb(name, shape, dt):
            return ctx.enter_context(nc.sbuf_tensor(name, shape, dt))

        def pb(name, shape, dt):
            return ctx.enter_context(nc.psum_tensor(name, shape, dt))

        def sem(name):
            return ctx.enter_context(nc.semaphore(name))

        ident = sb("ident", [P, P], fp32)
        ident_b = sb("ident_b", [P, P], bf16)
        ones = sb("ones", [P, P], fp32)
        select = sb("select", [P, H, P], bf16)
        weight = [sb(f"weight{l}", [P, F, D], fp32) for l in range(2)]
        score_w = [sb(f"score_w{l}", [P, F, 2 * H], fp32) for l in range(2)]
        score_b = sb("score_b", [P, 2, 2 * H], fp32)
        half_neg = sb("half_neg", [P, PAIR], fp32)
        xs = [sb(f"xs{p}", [P, T, D], fp32) for p in range(2)]
        mask = [sb(f"mask{p}", [P, T, N], fp8) for p in range(2)]
        adj_rows = sb("adj_rows", [P, 2, N], bf16)
        xT = sb("xT", [P, 2, F, P], fp32)
        h_ones = [sb(f"h_ones{q}", [P, T, H, KD], fp32) for q in range(2)]
        sd = [sb(f"sd{q}", [P, T, 2 * H], fp32) for q in range(2)]
        sT = [sb(f"sT{q}", [P, N], bf16) for q in range(2)]
        s_parts = sb("s_parts", [P, T, P], bf16)
        s_rest = sb("s_rest", [P, T, H], fp32)
        d_max = sb("d_max", [P, P], fp32)
        d_maxT = sb("d_maxT", [P, 1], fp32)
        d_diag = sb("d_diag", [P, H], fp32)
        d_top = sb("d_top", [P, H], fp32)
        zt = sb("zt", [P, T, H], fp32)
        args = sb("args", [P, 4, T, H], fp32)
        uvpq = [sb(f"uvpq{q}", [P, 4, T, H], fp32) for q in range(2)]
        h_sum = sb("h_sum", [P, D], fp32)
        h_mean = [sb(f"h_mean{q}", [P, H, K], fp32) for q in range(2)]
        neg = [sb(f"neg{k}", [P, T, N], fp8) for k in range(2)]
        pos = [sb(f"pos{k}", [P, T, N], fp8) for k in range(2)]
        y = sb("y", [P, 2, T, KD], fp32)
        y_parts = [sb(f"y_parts{k}", [P, 2, T, PARTS, KD], bf16) for k in range(2)]
        sums = [sb(f"sums{k}", [P, T, 2, KD], fp32) for k in range(2)]
        den = [sb(f"den{k}", [P, 3, T], fp32) for k in range(2)]
        o = sb("o", [P, T, D], fp32)
        stats = sb("stats", [P, T, 6], fp32)
        mv = sb("mv", [P, T, 2], fp32)
        rstd = sb("rstd", [P, T], fp32)
        shift = sb("shift", [P, T], fp32)
        staged = sb("staged", [P, 2, 2, D], fp32)

        s_ps = pb("s_ps", [P, N], fp32)
        acc = [pb(f"acc{k}", [P, 512], fp32) for k in range(ACCS)]
        misc = pb("misc", [P, 512], fp32)
        misc_b = misc[:, :].bitcast(bf16).rearrange("p (t n) -> p t n", t=T)
        wide = pb("wide", [P, 512], fp32)

        const_in = sem("const_in")
        w_in = sem("w_in")
        att_in = sem("att_in")
        x_in = [[sem(f"x_in{p}{k}") for k in range(PAIRS)] for p in range(2)]
        adj_in = [sem(f"adj_in{k}") for k in range(2)]
        out_stored = [sem(f"out_stored{k}") for k in range(2)]
        setup_dve = sem("setup_dve")
        setup_pool = sem("setup_pool")
        passed = sem("passed")
        s_rows = sem("s_rows")
        attended = sem("attended")
        xT_ps = sem("xT_ps")
        h_ps = sem("h_ps")
        sd_ps = sem("sd_ps")
        mask_ps = sem("mask_ps")
        guard_ps = sem("guard_ps")
        sT_ps = sem("sT_ps")
        mean_ps = sem("mean_ps")
        signed = sem("signed")
        xT_copied = sem("xT_copied")
        h_copied = sem("h_copied")
        exps = sem("exps")
        mean_copied = sem("mean_copied")
        rounded = sem("rounded")
        applied = sem("applied")
        acc_read = sem("acc_read")
        neg_made = sem("neg_made")
        edges = sem("edges")
        rest = sem("rest")
        middle = sem("middle")
        sd_copied = sem("sd_copied")
        mask_copied = sem("mask_copied")
        guard = sem("guard")
        sT_made = sem("sT_made")
        sT_copied = sem("sT_copied")
        dens = sem("dens")
        residual = sem("residual")
        normed = sem("normed")
        scaled = sem("scaled")
        rest_v = sem("rest_v")
        combined = sem("combined")
        summed = sem("summed")
        rstds = sem("rstds")

        GUARD = 6

        def wait(eng, s, value):
            if not isinstance(value, int) or value > 0:
                eng.wait_ge(s, value)

        def stand_apart(eng):
            eng.sem_inc(passed, 1)

        def phases(eng, phase):
            phase(-1, 3)
            phase(0, 0)
            loops = B // 2 - 1
            with eng.Fori(0, loops) as i:
                for phi in (1, 2, 3):
                    phase(i, phi)
                phase(i + 1, 0)
            for phi in (1, 2, 3):
                phase(loops, phi)
            phase(loops + 1, 0)

        def parts_of(pair, phi):
            if not isinstance(pair, int):
                return True, True, True
            u = 4 * pair + phi
            return 0 <= u < UNITS, u + 1 < UNITS, u - 1 >= 0

        def next_phase(pair, phi):
            return (pair, phi + 1) if phi < 3 else (pair + 1, 0)

        def prev_phase(pair, phi):
            return (pair, phi - 1) if phi > 0 else (pair - 1, 3)

        def graph_of(pair, phi):
            return 2 * pair + phi % 2

        def mask_graph(pair, phi):
            return graph_of(*next_phase(pair, phi)) if phi in (0, 3) else None

        MASK_AT = [(0, 3), (2, 2), (3, 2), (3, 7), (4, 3), (4, 7), (5, 5), (6, 7)]
        TURN_AT = [(2, 5), (3, 0), (3, 3), (3, 6), (4, 1), (4, 4), (5, 0), (5, 3)]
        PROJECT_AT = [(2, 7), (3, 2), (3, 5), (3, 7), (4, 3), (4, 6), (5, 2), (5, 5)]

        def job(places, h, it):
            return places.index((h, it)) if (h, it) in places else None

        def heads_ahead(pair, phi, h):
            attn, prep, _ = parts_of(pair, phi)
            if h < H - 1:
                return (pair, phi, h + 1) if attn else None
            return (*next_phase(pair, phi), 0) if prep else None

        def head_behind(pair, phi, h):
            attn, _, ends = parts_of(pair, phi)
            if h > 0:
                return (pair, phi, h - 1) if attn else None
            return (*prev_phase(pair, phi), H - 1) if ends else None

        def unit(pair, phi):
            return 4 * pair + phi

        block = ctx.enter_context(nc.Block())

        @block.sync
        def _(sp):
            sp.dma_start(ident[:, :], ident_in).then_inc(const_in, 16)
            sp.dma_start(select[:, :, :].bitcast(mybir.dt.uint16), select_in).then_inc(const_in, 16)
            sp.dma_start(weight[0][:, :, :], W0.rearrange("(k p) o -> p k o", p=P)).then_inc(w_in, 16)
            for k in range(F):
                sp.dma_start(weight[1][:, k, :].rearrange("p (h o) -> p h o", h=H),
                             W1[:, k * P:(k + 1) * P, :].rearrange("h p o -> p h o")).then_inc(w_in, 16)
            for n, v in enumerate((att0[:, 0:K], att0[:, K:2 * K], a1, a2)):
                sp.dma_start(o[:, n, :].rearrange("p (h o) -> p h o", h=H),
                             v.rearrange("(a h) o -> a h o", a=1).to_broadcast([P, H, K])).then_inc(att_in, 16)
            sp.dma_start(score_b[:, 0, 0:H], b0.rearrange("(a h) -> a h", a=1).to_broadcast([P, H]))\
              .then_inc(att_in, 16)

            def load_x(g, p, k):
                tiles = slice(k * PAIR, (k + 1) * PAIR)
                src = x[bass.ds(g, 1)].rearrange("a (t p) d -> p (a t) d", p=P)
                sp.dma_start(xs[p][:, tiles, :], src[:, tiles, :]).then_inc(x_in[p][k], 16)

            for k in range(PAIRS):
                load_x(0, 0, k)

            def phase(pair, phi):
                attn, prep, ends = parts_of(pair, phi)
                done = T * unit(*prev_phase(pair, phi))
                g = graph_of(*prev_phase(pair, phi))
                final = ends and phi in (0, 3)
                for k in range(PAIRS):
                    if final:
                        wait(sp, applied, done + 2 * (k + 1))
                        dst = out[bass.ds(g, 1)].rearrange("a (t p) d -> p (a t) d", p=P)
                        sp.dma_start(dst[:, 2 * k:2 * k + 2, :], staged[:, k % 2, :, :])\
                          .then_inc(out_stored[k % 2], 16)
                    if prep and attn and phi in (0, 3):
                        load_x(mask_graph(pair, phi), (phi + 1) % 2, k)

            phases(sp, phase)
            for k in range(2):
                sp.wait_ge(out_stored[k], 16 * (2 * B + 1))

        @block.gpsimd
        def _(pool):
            def load_adj(g, it):
                src = adj[bass.ds(g, 1)].rearrange("a (t p) j -> p (a t) j", p=P)
                pool.dma_start(adj_rows[:, it % 2, :], src[:, it, :]).then_inc(adj_in[it % 2], 16)

            nc.gpsimd.memset(half_neg[:, :], -0.5).then_inc(setup_pool, 1)
            nc.gpsimd.memset(h_ones[0][:, :, :, K:KD], 1.0).then_inc(setup_pool, 1)
            nc.gpsimd.memset(h_ones[1][:, :, :, K:KD], 1.0).then_inc(setup_pool, 1)
            pool.wait_ge(setup_pool, 3)
            load_adj(0, 0)
            load_adj(0, 1)

            def scale_head(pair, phi, h):
                u, q = unit(pair, phi), phi % 2
                g = H * u + h
                if h == 0:
                    pool.wait_ge(exps, u + 1)
                    pool.wait_ge(h_copied, T * (u + 1))
                for k in range(2):
                    wait(pool, rest, 3 * g - 1 + k)
                    factor = uvpq[q][:, 2 + k, :, h:h + 1].to_broadcast([P, T, KD])
                    nc.gpsimd.tensor_tensor(y[:, k], h_ones[q][:, :, h, :], factor, ALU.mult).then_inc(scaled, 1)

            def rest_of_v(pair, phi, h):
                g = H * unit(pair, phi) + h
                pool.wait_ge(rounded, 2 * g + 1)
                nc.gpsimd.tensor_tensor(y[:, 0], y[:, 0], y_parts[h % 2][:, 0, :, 0, :], ALU.subtract)\
                  .then_inc(rest_v, 1)

            def combine_sums(pair, phi, h):
                u, q = unit(pair, phi), phi % 2
                g = H * u + h
                s = sums[h % 2]
                pool.wait_ge(acc_read, T * (g + 1))
                for k in range(2):
                    factor = uvpq[q][:, k, :, h:h + 1].to_broadcast([P, T, KD])
                    nc.gpsimd.tensor_tensor(s[:, :, k, :], s[:, :, k, :], factor, ALU.mult).then_inc(combined, 1)
                pool.wait_ge(combined, 6 * g + 2)
                nc.gpsimd.tensor_tensor(s[:, :, 0, :], s[:, :, 0, :], s[:, :, 1, :], ALU.add).then_inc(combined, 1)

            def divide_sums(pair, phi, h):
                u, q = unit(pair, phi), phi % 2
                g = H * u + h
                s, r = sums[h % 2], den[h % 2]
                o_h, fill = o[:, :, h * K:(h + 1) * K], s[:, :, 1, 0:K]
                pool.wait_ge(dens, 3 * g + 3)
                if h == 0:
                    wait(pool, residual, T * u)
                    pool.wait_ge(mean_copied, u + 1)
                nc.gpsimd.tensor_tensor(fill, r[:, 0:1, :].rearrange("p a t -> p t a").to_broadcast([P, T, K]),
                                        h_mean[q][:, h:h + 1, :].to_broadcast([P, T, K]), ALU.mult)\
                  .then_inc(combined, 1)
                nc.gpsimd.tensor_tensor(o_h, s[:, :, 0, 0:K],
                                        r[:, 2:3, :].rearrange("p a t -> p t a").to_broadcast([P, T, K]), ALU.mult)\
                  .then_inc(combined, 1)
                pool.wait_ge(combined, 6 * g + 5)
                nc.gpsimd.tensor_tensor(o_h, o_h, fill, ALU.add).then_inc(combined, 1)

            def rstd_pair(pair, phi, k):
                n = PAIRS * unit(pair, phi) + k
                tiles = slice(k * PAIR, (k + 1) * PAIR)
                pool.wait_ge(normed, 2 * PAIR * (n + 1))
                stand_apart(pool)
                nc.gpsimd.tensor_scalar(rstd[:, tiles], mv[:, tiles, 1], EPS, None, ALU.add).then_inc(rstds, 1)
                nc.gpsimd.tensor_scalar(shift[:, tiles], mv[:, tiles, 0], -1.0, None, ALU.mult).then_inc(rstds, 1)
                pool.wait_ge(rstds, 4 * n + 1)
                nc.gpsimd.tensor_tensor(rstd[:, tiles], rstd[:, tiles], half_neg[:, :], ALU.pow).then_inc(rstds, 1)
                pool.wait_ge(rstds, 4 * n + 3)
                nc.gpsimd.tensor_tensor(shift[:, tiles], shift[:, tiles], rstd[:, tiles], ALU.mult).then_inc(rstds, 1)

            def sum_tile(pair, phi, t):
                u, q = unit(pair, phi), phi % 2
                if t == 0:
                    return
                pool.wait_ge(h_copied, T * u + t + 1)
                if t == 1:
                    wait(pool, mean_ps, u)
                else:
                    pool.wait_ge(summed, (T - 1) * u + t - 1)
                first = h_ones[q][:, 0, :, 0:K] if t == 1 else h_sum[:, :].rearrange("p (h o) -> p h o", h=H)
                nc.gpsimd.tensor_tensor(h_sum[:, :].rearrange("p (h o) -> p h o", h=H), first,
                                        h_ones[q][:, t, :, 0:K], ALU.add).then_inc(summed, 1)

            def phase(pair, phi):
                attn, prep, ends = parts_of(pair, phi)
                if phi == 1 and not (isinstance(pair, int) and pair == B // 2 - 1):
                    pool.wait_ge(mask_ps, T * (2 * pair + 2))
                    for it in range(2):
                        load_adj(2 * pair + 2, it)
                for h in range(H):
                    ahead, behind = heads_ahead(pair, phi, h), head_behind(pair, phi, h)
                    norm = prev_phase(pair, phi) if ends and h in (2, 3) else None
                    if ahead:
                        scale_head(*ahead)
                    if norm and h == 2:
                        rstd_pair(*norm, 0)
                    if behind:
                        combine_sums(*behind)
                    if ahead:
                        rest_of_v(*ahead)
                    if norm and h == 3:
                        rstd_pair(*norm, 2)
                    if behind:
                        divide_sums(*behind)
                    if norm:
                        rstd_pair(*norm, 1 if h == 2 else 3)
                    for it in range(T):
                        if prep and job(PROJECT_AT, h, it) is not None:
                            sum_tile(*next_phase(pair, phi), job(PROJECT_AT, h, it))
                        t = job(MASK_AT, h, it)
                        if prep and phi in (0, 3) and t is not None and (t < T - 2 or phi == 3):
                            g = mask_graph(pair, phi)
                            pool.wait_ge(mask_ps, T * g + t + 1)
                            load_adj(g if t < T - 2 else g + 1, (t + 2) % T)

            phases(pool, phase)

        @block.scalar
        def _(act):
            def sign_tile(pair, phi, h, t):
                u, q = unit(pair, phi), phi % 2
                g = H * u + h
                if t == 0:
                    act.wait_ge(s_rows, g + 1)
                    act.wait_ge(sd_copied, T * (u + 1))
                    wait(act, attended, T * (g - 1))
                    stand_apart(act)
                nc.scalar.activation(neg[h % 2][:, t, :], s_ps[:, :], ACT.Sign,
                                     bias=sd[q][:, t, H + h:H + h + 1], saturate=False).then_inc(signed, 1)

            def high_part(pair, phi, h, k):
                g = H * unit(pair, phi) + h
                act.wait_ge(scaled, 2 * g + k + 1)
                nc.scalar.activation(y_parts[h % 2][:, k, :, 0, :], y[:, k], ACT.Copy).then_inc(rounded, 1)

            def copy_xT(pair, phi, t):
                n = T * unit(pair, phi) + t
                act.wait_ge(xT_ps, n + 1)
                wait(act, sd_ps, n - 1)
                nc.scalar.activation(xT[:, t % 2], misc[:, :].rearrange("p (k n) -> p k n", k=F), ACT.Copy)\
                  .then_inc(xT_copied, 1)

            def copy_h(pair, phi, t):
                act.wait_ge(h_ps, T * unit(pair, phi) + t + 1)
                nc.scalar.activation(h_ones[phi % 2][:, t, :, 0:K], wide[:, :].rearrange("p (h o) -> p h o", h=H),
                                     ACT.Copy).then_inc(h_copied, 1)

            def apply_tile(pair, phi, t):
                u, p = unit(pair, phi), phi % 2
                k = t // PAIR
                dst = xs[p][:, t, :] if phi < 2 else staged[:, k % 2, t % PAIR, :]
                if t % PAIR == 0:
                    act.wait_ge(rstds, 4 * (PAIRS * u + k + 1))
                if phi >= 2 and t % PAIR == 0:
                    act.wait_ge(out_stored[k % 2], 16 * (2 * graph_of(pair, phi) + k // 2 + 1))
                nc.scalar.activation(dst, xs[p][:, t, :], ACT.Identity, bias=shift[:, t:t + 1], scale=rstd[:, t:t + 1])\
                  .then_inc(applied, 1)

            SIGNS = {0: (0, 1), 1: (2,), 2: (3,), 3: (4,), 4: (5,), 5: (6,), 6: (7,)}
            HIGH = {1: 0, 2: 1}
            APPLY = {(2, 3): 0, (3, 0): 1, (3, 5): 2, (4, 0): 3}

            def phase(pair, phi):
                _, prep, ends = parts_of(pair, phi)
                nxt = next_phase(pair, phi)
                for h in range(H):
                    ahead = heads_ahead(pair, phi, h)
                    for it in range(T):
                        if h == 6 and it == 5 and prep:
                            act.wait_ge(guard, GUARD * (unit(*nxt) + 1))
                            nc.scalar.activation(uvpq[nxt[1] % 2][:, :, :, :], args[:, :, :, :], ACT.Exp)\
                              .then_inc(exps, 1)
                        if ahead:
                            for t in SIGNS.get(it, ()):
                                sign_tile(*ahead, t)
                            if it in HIGH:
                                high_part(*ahead, HIGH[it])
                        if ends and (h, it) in APPLY:
                            for k in range(PAIR):
                                apply_tile(*prev_phase(pair, phi), PAIR * APPLY[h, it] + k)
                        if prep and job(TURN_AT, h, it) is not None:
                            copy_xT(*nxt, job(TURN_AT, h, it))
                        if prep and job(PROJECT_AT, h, it) is not None:
                            copy_h(*nxt, job(PROJECT_AT, h, it))
                    if h == 7 and prep:
                        act.wait_ge(mean_ps, unit(*nxt) + 1)
                        nc.scalar.activation(h_mean[nxt[1] % 2][:, :, :],
                                             wide[:, :].rearrange("p (h o) -> p h o", h=H), ACT.Copy,
                                             scale=1.0 / N).then_inc(mean_copied, 1)

            act.wait_ge(setup_pool, 3)
            phases(act, phase)

        @block.vector
        def _(dve):
            chain = [0]

            def link(ins):
                chain[0] += 1
                ins.then_inc(setup_dve, 1)
                dve.wait_ge(setup_dve, chain[0])

            nc.vector.memset(ones[:, :], 1.0)
            for k in range(2):
                nc.vector.memset(staged[:, k, :, :], 0.0).then_inc(out_stored[k], 16)
            nc.vector.memset(d_max[:, :], 0.0)
            nc.vector.memset(s_parts[:, :, :], 0.0)
            link(nc.vector.memset(score_b[:, 1, :], 0.0))
            link(nc.vector.memset(score_b[:, 0, H:2 * H], 0.0))
            dve.wait_ge(const_in, 32)
            link(nc.vector.tensor_copy(ident_b[:, :], ident[:, :]))
            dve.wait_ge(w_in, 16 * (1 + F))
            dve.wait_ge(att_in, 16 * 5)
            for l in range(2):
                for n in range(2):
                    vec = o[:, 2 * l + n, :].rearrange("p (a c) -> p a c", a=1).to_broadcast([P, F, D])
                    tmp = o[:, 4:4 + F, :]
                    link(nc.vector.tensor_tensor(tmp, weight[l][:, :, :], vec, ALU.mult))
                    link(nc.vector.tensor_reduce(score_w[l][:, :, n * H:(n + 1) * H],
                                                 tmp.rearrange("p k (h o) -> p k h o", h=H), AX.X, ALU.add))

            def read_acc(pair, phi, h, it):
                g = H * unit(pair, phi) + h
                dve.wait_ge(attended, T * g + it + 1)
                if it == 0:
                    wait(dve, combined, 6 * (g - 1))
                nc.vector.tensor_reduce(sums[h % 2][:, it],
                                        acc[it % ACCS][:, 0:2 * W3].rearrange("p (k s c) -> p k c s", k=2, s=PARTS),
                                        AX.X, ALU.add).then_inc(acc_read, 1)

            def make_edges(pair, phi, h, c):
                g = H * unit(pair, phi) + h
                tiles = slice(c * CHUNK, (c + 1) * CHUNK)
                n32, p32, m32 = (b[:, tiles, :].bitcast(int32) for b in (neg[h % 2], pos[h % 2], mask[phi % 2]))
                dve.wait_ge(signed, T * g + CHUNK * (c + 1))
                if phi < 2 and h == 0 and c == 0:
                    dve.wait_ge(mask_copied, T * (graph_of(pair, phi) + 1))
                nc.vector.scalar_tensor_tensor(n32, n32, SIGN_TO_EDGE, m32, ALU.logical_shift_right,
                                               ALU.bitwise_and).then_inc(neg_made, 1)
                dve.wait_ge(neg_made, NCHUNK * g + c + 1)
                nc.vector.tensor_tensor(p32, n32, m32, ALU.bitwise_xor).then_inc(edges, 1)

            def rest_of_q(pair, phi, h):
                g = H * unit(pair, phi) + h
                dve.wait_ge(rounded, 2 * g + 2)
                nc.vector.tensor_tensor(y[:, 1], y[:, 1], y_parts[h % 2][:, 1, :, 0, :], ALU.subtract)\
                  .then_inc(rest, 1)

            def middle_part(pair, phi, h, k):
                g = H * unit(pair, phi) + h
                if k == 0:
                    dve.wait_ge(rest_v, g + 1)
                else:
                    dve.wait_ge(rest, 3 * g + 1)
                nc.vector.tensor_copy(y_parts[h % 2][:, k, :, 1, :], y[:, k]).then_inc(middle, 1)

            def low_part(pair, phi, h, k):
                g = H * unit(pair, phi) + h
                yp = y_parts[h % 2]
                dve.wait_ge(middle, 2 * g + 2 - k)
                nc.vector.tensor_tensor(yp[:, k, :, 2, :], y[:, k], yp[:, k, :, 1, :], ALU.subtract).then_inc(rest, 1)

            def denominators(pair, phi, h):
                g = H * unit(pair, phi) + h
                s, r = sums[h % 2], den[h % 2]
                dve.wait_ge(combined, 6 * g + 3)
                nc.vector.tensor_scalar(r[:, 0, :], s[:, :, 0, K], 0.0, None, ALU.is_equal).then_inc(dens, 1)
                dve.wait_ge(dens, 3 * g + 1)
                nc.vector.tensor_tensor(r[:, 1, :], s[:, :, 0, K], r[:, 0, :], ALU.add).then_inc(dens, 1)
                dve.wait_ge(dens, 3 * g + 2)
                nc.vector.reciprocal(r[:, 2, :], r[:, 1, :]).then_inc(dens, 1)

            def add_residual(pair, phi, t):
                u, p = unit(pair, phi), phi % 2
                if t == 0:
                    dve.wait_ge(combined, 6 * H * (u + 1))
                if phi < 2:
                    nc.vector.scalar_tensor_tensor(xs[p][:, t, :], o[:, t, :], 0.0, xs[p][:, t, :], ALU.max, ALU.add)\
                      .then_inc(residual, 1)
                else:
                    nc.vector.tensor_tensor(xs[p][:, t, :], o[:, t, :], xs[p][:, t, :], ALU.add).then_inc(residual, 1)

            def norm_tile(pair, phi, t):
                n = T * unit(pair, phi) + t
                dve.wait_ge(residual, n + 1)
                nc.vector.bn_stats(stats[:, t, :], xs[phi % 2][:, t, :]).then_inc(normed, 1)
                dve.wait_ge(normed, 2 * n + 1)
                stand_apart(dve)
                nc.vector.bn_aggr(mv[:, t, :], stats[:, t, :]).then_inc(normed, 1)

            def copy_sd(pair, phi, t):
                u = unit(pair, phi)
                dve.wait_ge(sd_ps, T * u + t + 1)
                nc.vector.tensor_tensor(sd[phi % 2][:, t, :], misc[:, 0:2 * H], score_b[:, phi // 2, :], ALU.add)\
                  .then_inc(sd_copied, 1)

            def copy_mask(g, p, it):
                dve.wait_ge(mask_ps, T * g + it + 1)
                stand_apart(dve)
                nc.vector.tensor_scalar(mask[p][:, :, it * P:(it + 1) * P], misc_b, 0.0, EDGE, ALU.is_gt, ALU.mult, saturate=False)\
                  .then_inc(mask_copied, 1)

            def guard_a(pair, phi):
                u, q = unit(pair, phi), phi % 2
                s, d = sd[q][:, :, 0:H], sd[q][:, :, H:2 * H]
                dve.wait_ge(sd_copied, T * (u + 1))
                nc.vector.tensor_reduce(d_max[:, 0:H], d.rearrange("p t h -> p h t"), AX.X, ALU.max)\
                  .then_inc(guard, 1)
                nc.vector.tensor_copy(s_parts[:, :, 0:H], s).then_inc(sT_made, 1)
                dve.wait_ge(sT_made, 4 * u + 1)
                nc.vector.tensor_tensor(s_rest[:, :, :], s, s_parts[:, :, 0:H], ALU.subtract).then_inc(sT_made, 1)
                dve.wait_ge(sT_made, 4 * u + 2)
                nc.vector.tensor_copy(s_parts[:, :, H:2 * H], s_rest[:, :, :]).then_inc(sT_made, 1)
                dve.wait_ge(sT_made, 4 * u + 3)
                nc.vector.tensor_tensor(s_parts[:, :, 2 * H:3 * H], s_rest[:, :, :], s_parts[:, :, H:2 * H],
                                        ALU.subtract).then_inc(sT_made, 1)

            def guard_b(pair, phi):
                u = unit(pair, phi)
                dve.wait_ge(guard_ps, 2 * u + 1)
                nc.vector.tensor_reduce(d_maxT[:, :], misc[:, 0:P], AX.X, ALU.max).then_inc(guard, 1)
                dve.wait_ge(guard, GUARD * u + 2)
                nc.vector.tensor_scalar(d_diag[:, :], ident[:, 0:H], d_maxT[:, 0:1], None, ALU.mult)\
                  .then_inc(guard, 1)

            def guard_c(pair, phi):
                u, q = unit(pair, phi), phi % 2
                s, d = sd[q][:, :, 0:H], sd[q][:, :, H:2 * H]
                dve.wait_ge(guard_ps, 2 * u + 2)
                nc.vector.tensor_copy(d_top[:, :], misc[:, 0:H]).then_inc(guard, 1)
                dve.wait_ge(guard, GUARD * u + 4)
                top = d_top[:, :].rearrange("p (a h) -> p a h", a=1).to_broadcast([P, T, H])
                nc.vector.tensor_tensor(args[:, 2], d, top, ALU.subtract)
                nc.vector.tensor_tensor(zt[:, :, :], s, top, ALU.add).then_inc(guard, 1)
                dve.wait_ge(guard, GUARD * u + 5)
                nc.vector.tensor_scalar(args[:, 0], zt[:, :, :], 1.0 - SLOPE, 0.0, ALU.mult, ALU.min)
                nc.vector.tensor_scalar(args[:, 1], zt[:, :, :], SLOPE - 1.0, 0.0, ALU.mult, ALU.min)
                nc.vector.tensor_scalar(args[:, 3], args[:, 2], SLOPE, None, ALU.mult).then_inc(guard, 1)

            def copy_sT(pair, phi):
                dve.wait_ge(sT_ps, unit(pair, phi) + 1)
                nc.vector.tensor_copy(sT[phi % 2][:, :].rearrange("p (t n) -> p t n", t=T), misc_b)\
                  .then_inc(sT_copied, 1)

            EDGES = {1: 0, 3: 1, 5: 2, 7: 3}
            NORM = {(2, 0): 0, (2, 4): 1, (3, 1): 2, (3, 5): 3}

            def phase(pair, phi):
                attn, prep, ends = parts_of(pair, phi)
                nxt, prv = next_phase(pair, phi), prev_phase(pair, phi)
                for h in range(H):
                    ahead, behind = heads_ahead(pair, phi, h), head_behind(pair, phi, h)
                    for it in range(T):
                        if behind and it == 4:
                            denominators(*behind)
                        if ahead and it == 4:
                            rest_of_q(*ahead)
                            middle_part(*ahead, 1)
                        if ahead and it == 5:
                            middle_part(*ahead, 0)
                            low_part(*ahead, 0)
                        if ahead and it == 6:
                            low_part(*ahead, 1)
                        if ahead and it in EDGES:
                            make_edges(*ahead, EDGES[it])
                        if attn:
                            read_acc(pair, phi, h, it)
                        if ends and h == 1 and it < PAIRS:
                            for k in range(PAIR):
                                add_residual(*prv, PAIR * it + k)
                        if ends and (h, it) in NORM:
                            for k in range(PAIR):
                                norm_tile(*prv, PAIR * NORM[h, it] + k)
                        if prep and job(PROJECT_AT, h, it) is not None:
                            copy_sd(*nxt, job(PROJECT_AT, h, it))
                        if prep and phi in (0, 3) and job(MASK_AT, h, it) is not None:
                            copy_mask(mask_graph(pair, phi), (phi + 1) % 2, job(MASK_AT, h, it))
                        if prep and (h, it) == (5, 7):
                            guard_a(*nxt)
                        if prep and h == 6:
                            if it == 1:
                                guard_b(*nxt)
                            if it == 3:
                                guard_c(*nxt)
                            if it == 5:
                                copy_sT(*nxt)

            phases(dve, phase)

        @block.tensor
        def _(pe):
            def rows_of_s(pair, phi, h):
                u, q = unit(pair, phi), phi % 2
                g = H * u + h
                if h == 0:
                    pe.wait_ge(sT_copied, u + 1)
                wait(pe, signed, T * g)
                for k in range(2):
                    last = nc.tensor.matmul(s_ps[:, k * 512:(k + 1) * 512], select[:, h, :],
                                            sT[q][:, k * 512:(k + 1) * 512], start=True, stop=True)
                last.then_inc(s_rows, 1)

            def attend(pair, phi, h, it):
                g = H * unit(pair, phi) + h
                n = T * g + it
                wait(pe, acc_read, n - ACCS + 1)
                if it == 0:
                    pe.wait_ge(rest, 3 * g + 3)
                stand_apart(pe)
                cols = slice(it * P, (it + 1) * P)
                for k, edge in enumerate((pos[h % 2], neg[h % 2])):
                    for t in range(T):
                        if it == 0 and k == 0 and t % CHUNK == 0:
                            pe.wait_ge(edges, NCHUNK * g + t // CHUNK + 1)
                            stand_apart(pe)
                        last = nc.tensor.matmul(acc[it % ACCS][:, k * W3:(k + 1) * W3], edge[:, t, cols],
                                                y_parts[h % 2][:, k, t].rearrange("p s c -> p (s c)"),
                                                start=(t == 0), stop=(t == T - 1))
                last.then_inc(attended, 1)

            def transpose_mask(g, it):
                pe.wait_ge(adj_in[it % 2], 16 * (T // 2 * g + it // 2 + 1))
                for t in range(T):
                    last = nc.tensor.transpose(misc_b[:, t, :], adj_rows[:, it % 2, t * P:(t + 1) * P], ident_b[:, :])
                last.then_inc(mask_ps, 1)

            def transpose_x(pair, phi, t):
                u, p = unit(pair, phi), phi % 2
                if phi < 2:
                    if t % PAIR == 0:
                        pe.wait_ge(x_in[p][t // PAIR], 16 * (pair + 1))
                else:
                    pe.wait_ge(applied, T * (u - 2) + t + 1)
                for k in range(F):
                    last = nc.tensor.transpose(misc[:, k * P:(k + 1) * P], xs[p][:, t, k * P:(k + 1) * P], ident[:, :])
                last.then_inc(xT_ps, 1)

            def project(pair, phi, t):
                u, l = unit(pair, phi), phi // 2
                n = T * u + t
                pe.wait_ge(xT_copied, n + 1)
                if t == 0:
                    wait(pe, mean_copied, u)
                else:
                    pe.wait_ge(h_copied, n)
                for k in range(F):
                    last = nc.tensor.matmul(wide[:, :], xT[:, t % 2, k, :], weight[l][:, k, :],
                                            start=(k == 0), stop=(k == F - 1))
                last.then_inc(h_ps, 1)
                for k in range(F):
                    last = nc.tensor.matmul(misc[:, 0:2 * H], xT[:, t % 2, k, :], score_w[l][:, k, :],
                                            start=(k == 0), stop=(k == F - 1))
                last.then_inc(sd_ps, 1)

            def phase(pair, phi):
                attn, prep, ends = parts_of(pair, phi)
                nxt = next_phase(pair, phi)
                u = unit(*nxt)
                empty = (mask_copied, T * (2 * pair + 1 + phi)) if phi < 2 else (sT_copied, u)
                for h in range(H):
                    ahead = heads_ahead(pair, phi, h)
                    for it in range(T):
                        if ahead and (h, it) == (H - 1, 0):
                            rows_of_s(*ahead)
                        if it == T - 1 and h != H - 2:
                            after = (pair, phi, h + 2) if h < H - 2 else (*nxt, 1)
                            if (attn if h < H - 2 else prep):
                                rows_of_s(*after)
                        if attn:
                            attend(pair, phi, h, it)
                        if not prep:
                            continue
                        if job(TURN_AT, h, it) is not None:
                            wait(pe, *empty)
                            transpose_x(*nxt, job(TURN_AT, h, it))
                        if job(PROJECT_AT, h, it) is not None:
                            t = job(PROJECT_AT, h, it)
                            project(*nxt, t)
                            empty = (sd_copied, T * u + t + 1)
                        if h == 6 and it == 0:
                            wait(pe, *empty)
                            pe.wait_ge(guard, GUARD * u + 1)
                            nc.tensor.transpose(misc[:, 0:P], d_max[:, :], ident[:, :]).then_inc(guard_ps, 1)
                        if h == 6 and it == 2:
                            pe.wait_ge(guard, GUARD * u + 3)
                            nc.tensor.matmul(misc[:, 0:H], ones[:, :], d_diag[:, :], start=True, stop=True)\
                              .then_inc(guard_ps, 1)
                        if h == 6 and it == 4:
                            pe.wait_ge(guard, GUARD * u + 4)
                            pe.wait_ge(sT_made, 4 * (u + 1))
                            for t in range(T):
                                last = nc.tensor.transpose(misc_b[:, t, :], s_parts[:, t, :], ident_b[:, :])
                            last.then_inc(sT_ps, 1)
                            empty = (sT_copied, u + 1)
                        if phi in (0, 3) and job(MASK_AT, h, it) is not None:
                            g, t = mask_graph(pair, phi), job(MASK_AT, h, it)
                            wait(pe, *empty)
                            transpose_mask(g, t)
                            empty = (mask_copied, T * g + t + 1)
                        if h == 7 and it == 3:
                            pe.wait_ge(summed, (T - 1) * (u + 1))
                            pe.wait_ge(h_copied, T * (u + 1))
                            nc.tensor.matmul(wide[:, :], ones[:, :], h_sum[:, :], start=True, stop=True)\
                              .then_inc(mean_ps, 1)

            pe.wait_ge(setup_dve, 3 + 8)
            phases(pe, phase)


def kernel(x, adj, L0_gnn_W_proj, L0_gnn_W_att, L0_gnn_b_att, L1_gnn_W, L1_gnn_a1, L1_gnn_a2):
    import concourse.bacc as bacc
    from concourse.bass_utils import run_bass_kernel_spmd

    nc = bacc.Bacc("TRN2", target_bir_lowering=False, num_devices=1)
    select = np.zeros((P, H, P), np.uint16)
    for part in range(PARTS):
        for h in range(H):
            select[part * H + h, h, :] = 0x3F80
    ins = {
        "x": np.ascontiguousarray(x), "adj": np.ascontiguousarray(adj), "W0": np.ascontiguousarray(L0_gnn_W_proj),
        "att0": np.ascontiguousarray(L0_gnn_W_att), "b0": np.ascontiguousarray(L0_gnn_b_att),
        "W1": np.ascontiguousarray(L1_gnn_W), "a1": np.ascontiguousarray(L1_gnn_a1),
        "a2": np.ascontiguousarray(L1_gnn_a2), "ident": np.eye(P, dtype=np.float32), "select": select,
    }
    aps = [nc.dram_tensor(f"in_{n}", a.shape, mybir.dt.from_np(a.dtype), kind="ExternalInput").ap()
           for n, a in ins.items()]
    out = nc.dram_tensor("out_x", (B, N, D), fp32, kind="ExternalOutput").ap()
    gat_two_layers(nc, *aps, out)
    r = run_bass_kernel_spmd(nc, [{f"in_{n}": a for n, a in ins.items()}], core_ids=[0])
    return r.results[0]["out_x"]
```

```python
import numpy as np

import concourse.bass as bass
from concourse import mybir
from contextlib import ExitStack

fp32 = mybir.dt.float32
bf16 = mybir.dt.bfloat16
fp8 = mybir.dt.float8e4
int32 = mybir.dt.int32
ALU = mybir.AluOpType
ACT = mybir.ActivationFunctionType
AX = mybir.AxisListType

P = 128
B, N, D = 16, 1024, 512
H, K = 8, 64
T = N // P
F = D // P
KD = K + 1
PARTS = 3
W3 = PARTS * KD
UNITS = 2 * B
SLOPE = 0.2
EPS = 1e-5
TINY = 2.0 ** -126
EDGE = 2.0 ** -6
SIGN_TO_EDGE = 4
CHUNK = 2
NCHUNK = T // CHUNK
PAIR = 2
PAIRS = T // PAIR
HALF = D // 2
ACCS = 4
assert H * K == D


def gat_two_layers(nc, x, adj, W0, att0, b0, W1, a1, a2, ident_in, select_in, out):
    ctx = ExitStack()
    with ctx:
        def sb(name, shape, dt):
            return ctx.enter_context(nc.sbuf_tensor(name, shape, dt))

        def pb(name, shape, dt):
            return ctx.enter_context(nc.psum_tensor(name, shape, dt))

        def sem(name):
            return ctx.enter_context(nc.semaphore(name))

        ident = sb("ident", [P, P], fp32)
        ident_b = sb("ident_b", [P, P], bf16)
        ones = sb("ones", [P, P], fp32)
        select = sb("select", [P, H, P], bf16)
        weight = [sb(f"weight{l}", [P, F, D + 2 * H], fp32) for l in range(2)]
        score_w = [w[:, :, HALF:HALF + 2 * H] for w in weight]
        att_vec = sb("att_vec", [P, 4, D], fp32)
        score_b = sb("score_b", [P, 2, H], fp32)
        half_neg = sb("half_neg", [P, PAIR], fp32)
        xs = [sb(f"xs{p}", [P, T, D], fp32) for p in range(2)]
        mask = [sb(f"mask{p}", [P, T, N], fp8) for p in range(2)]
        adj_rows = sb("adj_rows", [P, 2, N], bf16)
        xT = sb("xT", [P, 2, F, P], fp32)
        h_ones = [sb(f"h_ones{q}", [P, T, H, KD], fp32) for q in range(2)]
        sd = [sb(f"sd{q}", [P, T, 2 * H], fp32) for q in range(2)]
        sT = [sb(f"sT{q}", [P, N], bf16) for q in range(2)]
        s_parts = sb("s_parts", [P, T, P], bf16)
        s_rest = sb("s_rest", [P, T, H], fp32)
        d_max = sb("d_max", [P, P], fp32)
        d_maxT = sb("d_maxT", [P, 1], fp32)
        d_diag = sb("d_diag", [P, H], fp32)
        d_top = sb("d_top", [P, H], fp32)
        zt = sb("zt", [P, T, H], fp32)
        args = sb("args", [P, 4, T, H], fp32)
        uvpq = [sb(f"uvpq{q}", [P, 4, T, H], fp32) for q in range(2)]
        h_sum = sb("h_sum", [P, D], fp32)
        h_mean = [sb(f"h_mean{q}", [P, H, K], fp32) for q in range(2)]
        neg = [sb(f"neg{k}", [P, T, N], fp8) for k in range(2)]
        pos = [sb(f"pos{k}", [P, T, N], fp8) for k in range(2)]
        y = sb("y", [P, 2, T, KD], fp32)
        y_parts = [sb(f"y_parts{k}", [P, 2, T, PARTS, KD], bf16) for k in range(2)]
        sums = [sb(f"sums{k}", [P, T, 2, KD], fp32) for k in range(2)]
        den = [sb(f"den{k}", [P, 3, T], fp32) for k in range(2)]
        o = [sb(f"o{k}", [P, T, K], fp32) for k in range(2)]
        stats = sb("stats", [P, T, 6], fp32)
        mv = sb("mv", [P, T, 2], fp32)
        rstd = sb("rstd", [P, T], fp32)
        shift = sb("shift", [P, T], fp32)
        staged = sb("staged", [P, 2, 2, D], fp32)

        s_ps = pb("s_ps", [P, N], fp32)
        acc = [pb(f"acc{k}", [P, 512], fp32) for k in range(ACCS)]
        misc = pb("misc", [P, 512], fp32)
        misc_b = misc[:, :].bitcast(bf16).rearrange("p (t n) -> p t n", t=T)
        wide = pb("wide", [P, 512], fp32)

        ident_loaded = sem("ident_loaded")
        select_loaded = sem("select_loaded")
        layer_in = [sem(f"layer_in{l}") for l in range(2)]
        x_in = [[sem(f"x_in{p}{k}") for k in range(PAIRS)] for p in range(2)]
        adj_in = [sem(f"adj_in{k}") for k in range(2)]
        out_stored = [sem(f"out_stored{k}") for k in range(2)]
        setup_dve = sem("setup_dve")
        setup_pool = sem("setup_pool")
        passed = sem("passed")
        s_rows = sem("s_rows")
        attended = sem("attended")
        xT_ps = sem("xT_ps")
        h_ps = sem("h_ps")
        mask_ps = sem("mask_ps")
        guard_ps = sem("guard_ps")
        sT_ps = sem("sT_ps")
        mean_ps = sem("mean_ps")
        signed = sem("signed")
        xT_copied = sem("xT_copied")
        half_copied = sem("half_copied")
        h_copied = sem("h_copied")
        exps = sem("exps")
        mean_copied = sem("mean_copied")
        rounded = sem("rounded")
        middle_q = sem("middle_q")
        applied = sem("applied")
        acc_read = sem("acc_read")
        neg_made = sem("neg_made")
        edges = sem("edges")
        rest = sem("rest")
        middle_v = sem("middle_v")
        mask_copied = sem("mask_copied")
        guard = sem("guard")
        sT_made = sem("sT_made")
        sT_copied = sem("sT_copied")
        dens = sem("dens")
        residual = sem("residual")
        normed = sem("normed")
        scaled = sem("scaled")
        rest_v = sem("rest_v")
        combined = sem("combined")
        summed = sem("summed")
        rstds = sem("rstds")

        GUARD = 6

        def wait(eng, s, value):
            if not isinstance(value, int) or value > 0:
                eng.wait_ge(s, value)

        def stand_apart(eng):
            eng.sem_inc(passed, 1)

        def phases(eng, phase):
            phase(-1, 3)
            phase(0, 0)
            loops = B // 2 - 1
            with eng.Fori(0, loops) as i:
                for phi in (1, 2, 3):
                    phase(i, phi)
                phase(i + 1, 0)
            for phi in (1, 2, 3):
                phase(loops, phi)
            phase(loops + 1, 0)

        def parts_of(pair, phi):
            if not isinstance(pair, int):
                return True, True, True
            u = 4 * pair + phi
            return 0 <= u < UNITS, u + 1 < UNITS, u - 1 >= 0

        def next_phase(pair, phi):
            return (pair, phi + 1) if phi < 3 else (pair + 1, 0)

        def prev_phase(pair, phi):
            return (pair, phi - 1) if phi > 0 else (pair - 1, 3)

        def graph_of(pair, phi):
            return 2 * pair + phi % 2

        def mask_graph(pair, phi):
            return graph_of(*next_phase(pair, phi)) if phi in (0, 3) else None

        MASK_AT = [(2, 7), (3, 2), (3, 7), (4, 3), (4, 7), (5, 2), (5, 5), (6, 7)]
        TURN_AT = [(2, 5), (3, 0), (3, 3), (3, 6), (4, 1), (4, 4), (5, 0), (5, 3)]
        PROJECT_AT = [(2, 7), (3, 2), (3, 5), (3, 7), (4, 3), (4, 6), (5, 2), (5, 5)]

        def job(places, h, it):
            return places.index((h, it)) if (h, it) in places else None

        def heads_ahead(pair, phi, h):
            attn, prep, _ = parts_of(pair, phi)
            if h < H - 1:
                return (pair, phi, h + 1) if attn else None
            return (*next_phase(pair, phi), 0) if prep else None

        def head_behind(pair, phi, h):
            attn, _, ends = parts_of(pair, phi)
            if h > 0:
                return (pair, phi, h - 1) if attn else None
            return (*prev_phase(pair, phi), H - 1) if ends else None

        def head_before(pair, phi, h):
            attn, _, ends = parts_of(pair, phi)
            if h > 1:
                return (pair, phi, h - 2) if attn else None
            return (*prev_phase(pair, phi), H - 2 + h) if ends else None

        def unit(pair, phi):
            return 4 * pair + phi

        block = ctx.enter_context(nc.Block())

        @block.sync
        def _(sp):
            def load_x(g, p, k):
                tiles = slice(k * PAIR, (k + 1) * PAIR)
                src = x[bass.ds(g, 1)].rearrange("a (t p) d -> p (a t) d", p=P)
                sp.dma_start(xs[p][:, tiles, :], src[:, tiles, :]).then_inc(x_in[p][k], 16)

            def by_head(vector):
                return vector.rearrange("(a h) o -> a h o", a=1).to_broadcast([P, H, K])

            def load_vector(l, n, vector):
                sp.dma_start(att_vec[:, 2 * l + n, :].rearrange("p (h o) -> p h o", h=H), by_head(vector))\
                  .then_inc(layer_in[l], 16)

            halves = (slice(0, HALF), slice(HALF + 2 * H, D + 2 * H))
            sp.dma_start(ident[:, :], ident_in).then_inc(ident_loaded, 16)
            load_x(0, 0, 0)
            for n, cols in enumerate(halves):
                sp.dma_start(weight[0][:, :, cols], W0.rearrange("(k p) o -> p k o", p=P)
                             [:, :, n * HALF:(n + 1) * HALF]).then_inc(layer_in[0], 16)
            load_vector(0, 0, att0[:, 0:K])
            load_vector(0, 1, att0[:, K:2 * K])
            sp.dma_start(score_b[:, 0, :], b0.rearrange("(a h) -> a h", a=1).to_broadcast([P, H]))\
              .then_inc(layer_in[0], 16)
            for k in range(1, PAIRS):
                load_x(0, 0, k)
            sp.dma_start(select[:, :, :].bitcast(mybir.dt.uint16), select_in).then_inc(select_loaded, 16)
            for k in range(F):
                for n, cols in enumerate(halves):
                    sp.dma_start(weight[1][:, k, cols].rearrange("p (h o) -> p h o", h=H // 2),
                                 W1[n * (H // 2):(n + 1) * (H // 2), k * P:(k + 1) * P, :]
                                 .rearrange("h p o -> p h o")).then_inc(layer_in[1], 16)
            load_vector(1, 0, a1)
            load_vector(1, 1, a2)

            def phase(pair, phi):
                attn, prep, ends = parts_of(pair, phi)
                done = T * unit(*prev_phase(pair, phi))
                g = graph_of(*prev_phase(pair, phi))
                final = ends and phi in (0, 3)
                for k in range(PAIRS):
                    if final:
                        wait(sp, applied, done + 2 * (k + 1))
                        dst = out[bass.ds(g, 1)].rearrange("a (t p) d -> p (a t) d", p=P)
                        sp.dma_start(dst[:, 2 * k:2 * k + 2, :], staged[:, k % 2, :, :])\
                          .then_inc(out_stored[k % 2], 16)
                    if prep and attn and phi in (0, 3):
                        load_x(mask_graph(pair, phi), (phi + 1) % 2, k)

            phases(sp, phase)
            for k in range(2):
                sp.wait_ge(out_stored[k], 16 * (2 * B + 1))

        @block.gpsimd
        def _(pool):
            def load_adj(g, it):
                src = adj[bass.ds(g, 1)].rearrange("a (t p) j -> p (a t) j", p=P)
                pool.dma_start(adj_rows[:, it % 2, :], src[:, it, :]).then_inc(adj_in[it % 2], 16)

            nc.gpsimd.memset(half_neg[:, :], -0.5).then_inc(setup_pool, 1)
            nc.gpsimd.memset(h_ones[0][:, :, :, K:KD], 1.0).then_inc(setup_pool, 1)
            nc.gpsimd.memset(h_ones[1][:, :, :, K:KD], 1.0).then_inc(setup_pool, 1)
            pool.wait_ge(setup_pool, 3)
            load_adj(0, 0)
            load_adj(0, 1)

            def scale_head(pair, phi, h):
                u, q = unit(pair, phi), phi % 2
                g = H * u + h
                if h == 0:
                    pool.wait_ge(exps, u + 1)
                    pool.wait_ge(h_copied, T * (u + 1))
                for k in range(2):
                    wait(pool, rest, 3 * g)
                    factor = uvpq[q][:, 2 + k, :, h:h + 1].to_broadcast([P, T, KD])
                    nc.gpsimd.tensor_tensor(y[:, k], h_ones[q][:, :, h, :], factor, ALU.mult).then_inc(scaled, 1)

            def rest_of_v(pair, phi, h):
                g = H * unit(pair, phi) + h
                pool.wait_ge(rounded, 2 * g + 1)
                nc.gpsimd.tensor_tensor(y[:, 0], y[:, 0], y_parts[h % 2][:, 0, :, 0, :], ALU.subtract)\
                  .then_inc(rest_v, 1)

            def combine_sums(pair, phi, h):
                u, q = unit(pair, phi), phi % 2
                g = H * u + h
                s = sums[h % 2]
                pool.wait_ge(acc_read, T * (g + 1))
                for k in range(2):
                    factor = uvpq[q][:, k, :, h:h + 1].to_broadcast([P, T, KD])
                    nc.gpsimd.tensor_tensor(s[:, :, k, :], s[:, :, k, :], factor, ALU.mult).then_inc(combined, 1)
                pool.wait_ge(combined, 6 * g + 2)
                nc.gpsimd.tensor_tensor(s[:, :, 0, :], s[:, :, 0, :], s[:, :, 1, :], ALU.add).then_inc(combined, 1)

            def divide_sums(pair, phi, h):
                u, q = unit(pair, phi), phi % 2
                g = H * u + h
                s, r = sums[h % 2], den[h % 2]
                o_h, fill = o[h % 2][:, :, :], s[:, :, 1, 0:K]
                pool.wait_ge(dens, 3 * g + 3)
                wait(pool, residual, g - 1)
                if h == 0:
                    pool.wait_ge(mean_copied, u + 1)
                nc.gpsimd.tensor_tensor(fill, r[:, 0:1, :].rearrange("p a t -> p t a").to_broadcast([P, T, K]),
                                        h_mean[q][:, h:h + 1, :].to_broadcast([P, T, K]), ALU.mult)\
                  .then_inc(combined, 1)
                nc.gpsimd.tensor_tensor(o_h, s[:, :, 0, 0:K],
                                        r[:, 2:3, :].rearrange("p a t -> p t a").to_broadcast([P, T, K]), ALU.mult)\
                  .then_inc(combined, 1)
                pool.wait_ge(combined, 6 * g + 5)
                nc.gpsimd.tensor_tensor(o_h, o_h, fill, ALU.add).then_inc(combined, 1)

            def rstd_pair(pair, phi, k):
                n = PAIRS * unit(pair, phi) + k
                tiles = slice(k * PAIR, (k + 1) * PAIR)
                pool.wait_ge(normed, 2 * PAIR * (n + 1))
                stand_apart(pool)
                nc.gpsimd.tensor_scalar(rstd[:, tiles], mv[:, tiles, 1], EPS, None, ALU.add).then_inc(rstds, 1)
                nc.gpsimd.tensor_scalar(shift[:, tiles], mv[:, tiles, 0], -1.0, None, ALU.mult).then_inc(rstds, 1)
                pool.wait_ge(rstds, 4 * n + 1)
                nc.gpsimd.tensor_tensor(rstd[:, tiles], rstd[:, tiles], half_neg[:, :], ALU.pow).then_inc(rstds, 1)
                pool.wait_ge(rstds, 4 * n + 3)
                nc.gpsimd.tensor_tensor(shift[:, tiles], shift[:, tiles], rstd[:, tiles], ALU.mult).then_inc(rstds, 1)

            def sum_tile(pair, phi, t):
                u, q = unit(pair, phi), phi % 2
                if t == 0:
                    return
                pool.wait_ge(h_copied, T * u + t + 1)
                if t == 1:
                    wait(pool, mean_ps, u)
                else:
                    pool.wait_ge(summed, (T - 1) * u + t - 1)
                first = h_ones[q][:, 0, :, 0:K] if t == 1 else h_sum[:, :].rearrange("p (h o) -> p h o", h=H)
                nc.gpsimd.tensor_tensor(h_sum[:, :].rearrange("p (h o) -> p h o", h=H), first,
                                        h_ones[q][:, t, :, 0:K], ALU.add).then_inc(summed, 1)

            def phase(pair, phi):
                attn, prep, ends = parts_of(pair, phi)
                if phi == 1 and not (isinstance(pair, int) and pair == B // 2 - 1):
                    pool.wait_ge(mask_ps, T * (2 * pair + 2))
                    for it in range(2):
                        load_adj(2 * pair + 2, it)
                for h in range(H):
                    ahead, behind = heads_ahead(pair, phi, h), head_behind(pair, phi, h)
                    norm = prev_phase(pair, phi) if ends and h in (2, 3) else None
                    if ahead:
                        scale_head(*ahead)
                    if norm:
                        rstd_pair(*norm, 0 if h == 2 else 2)
                    if behind:
                        combine_sums(*behind)
                    if ahead:
                        rest_of_v(*ahead)
                    if norm:
                        rstd_pair(*norm, 1 if h == 2 else 3)
                    if behind:
                        divide_sums(*behind)
                    for it in range(T):
                        if prep and job(PROJECT_AT, h, it) is not None:
                            sum_tile(*next_phase(pair, phi), job(PROJECT_AT, h, it))
                        t = job(MASK_AT, h, it)
                        if prep and phi in (0, 3) and t is not None and (t < T - 2 or phi == 3):
                            g = mask_graph(pair, phi)
                            pool.wait_ge(mask_ps, T * g + t + 1)
                            load_adj(g if t < T - 2 else g + 1, (t + 2) % T)

            phases(pool, phase)

        @block.scalar
        def _(act):
            def sign_tile(pair, phi, h, t):
                u, q = unit(pair, phi), phi % 2
                g = H * u + h
                if t == 0:
                    act.wait_ge(s_rows, g + 1)
                    act.wait_ge(h_copied, T * (u + 1))
                    wait(act, attended, T * (g - 1))
                    stand_apart(act)
                nc.scalar.activation(neg[h % 2][:, t, :], s_ps[:, :], ACT.Sign,
                                     bias=sd[q][:, t, H + h:H + h + 1], saturate=False).then_inc(signed, 1)

            def high_part(pair, phi, h, k):
                g = H * unit(pair, phi) + h
                act.wait_ge(scaled, 2 * g + k + 1)
                nc.scalar.activation(y_parts[h % 2][:, k, :, 0, :], y[:, k], ACT.Copy).then_inc(rounded, 1)

            def middle_part_q(pair, phi, h):
                g = H * unit(pair, phi) + h
                act.wait_ge(rest, 3 * g + 1)
                nc.scalar.activation(y_parts[h % 2][:, 1, :, 1, :], y[:, 1], ACT.Copy).then_inc(middle_q, 1)

            def copy_xT(pair, phi, t):
                n = T * unit(pair, phi) + t
                act.wait_ge(xT_ps, n + 1)
                wait(act, h_ps, 2 * (n - 1))
                nc.scalar.activation(xT[:, t % 2], misc[:, :].rearrange("p (k n) -> p k n", k=F), ACT.Copy)\
                  .then_inc(xT_copied, 1)

            def copy_h(pair, phi, t):
                n = T * unit(pair, phi) + t
                for k, bank, done in ((1, misc, half_copied), (0, wide, h_copied)):
                    heads = slice(k * (H // 2), (k + 1) * (H // 2))
                    act.wait_ge(h_ps, 2 * n + 2 - k)
                    if bank is wide:
                        nc.scalar.activation(sd[phi % 2][:, t, :], wide[:, HALF:HALF + 2 * H], ACT.Copy)
                    nc.scalar.activation(h_ones[phi % 2][:, t, heads, 0:K],
                                         bank[:, 0:HALF].rearrange("p (h o) -> p h o", h=H // 2), ACT.Copy)\
                      .then_inc(done, 1)

            def apply_tile(pair, phi, t):
                u, p = unit(pair, phi), phi % 2
                k = t // PAIR
                dst = xs[p][:, t, :] if phi < 2 else staged[:, k % 2, t % PAIR, :]
                if t % PAIR == 0:
                    act.wait_ge(rstds, 4 * (PAIRS * u + k + 1))
                if phi >= 2 and t % PAIR == 0:
                    act.wait_ge(out_stored[k % 2], 16 * (2 * graph_of(pair, phi) + k // 2 + 1))
                nc.scalar.activation(dst, xs[p][:, t, :], ACT.Identity, bias=shift[:, t:t + 1], scale=rstd[:, t:t + 1])\
                  .then_inc(applied, 1)

            SIGNS = {0: (0, 1), 2: (2,), 3: (3, 4), 4: (5,), 5: (6,), 6: (7,)}
            HIGH = {1: 0, 2: 1}
            APPLY = {(2, 1): 0, (2, 6): 1, (3, 2): 2, (3, 6): 3}

            def phase(pair, phi):
                _, prep, ends = parts_of(pair, phi)
                nxt = next_phase(pair, phi)
                for h in range(H):
                    ahead = heads_ahead(pair, phi, h)
                    for it in range(T):
                        if h == 6 and it == 5 and prep:
                            act.wait_ge(guard, GUARD * (unit(*nxt) + 1))
                            nc.scalar.activation(uvpq[nxt[1] % 2][:, :, :, :], args[:, :, :, :], ACT.Exp)\
                              .then_inc(exps, 1)
                        if ahead:
                            for t in SIGNS.get(it, ()):
                                sign_tile(*ahead, t)
                            if it in HIGH:
                                high_part(*ahead, HIGH[it])
                            if it == 4:
                                middle_part_q(*ahead)
                        if ends and (h, it) in APPLY:
                            for k in range(PAIR):
                                apply_tile(*prev_phase(pair, phi), PAIR * APPLY[h, it] + k)
                        if prep and job(TURN_AT, h, it) is not None:
                            copy_xT(*nxt, job(TURN_AT, h, it))
                        if prep and job(PROJECT_AT, h, it) is not None:
                            copy_h(*nxt, job(PROJECT_AT, h, it))
                    if h == 7 and prep:
                        act.wait_ge(mean_ps, unit(*nxt) + 1)
                        nc.scalar.activation(h_mean[nxt[1] % 2][:, :, :],
                                             wide[:, :].rearrange("p (h o) -> p h o", h=H), ACT.Copy,
                                             scale=1.0 / N).then_inc(mean_copied, 1)

            act.wait_ge(setup_pool, 3)
            phases(act, phase)

        @block.vector
        def _(dve):
            chain = [0]

            def link(ins):
                chain[0] += 1
                ins.then_inc(setup_dve, 1)
                dve.wait_ge(setup_dve, chain[0])

            nc.vector.memset(ones[:, :], 1.0)
            for k in range(2):
                nc.vector.memset(staged[:, k, :, :], 0.0).then_inc(out_stored[k], 16)
            nc.vector.memset(d_max[:, :], 0.0)
            nc.vector.memset(s_parts[:, :, :], 0.0)
            link(nc.vector.memset(score_b[:, 1, :], 0.0))
            dve.wait_ge(ident_loaded, 16)
            link(nc.vector.tensor_copy(ident_b[:, :], ident[:, :]))
            def score_weights(l, n, half):
                cols = slice(half * HALF, (half + 1) * HALF)
                w = weight[l][:, :, 0:HALF] if half == 0 else weight[l][:, :, HALF + 2 * H:D + 2 * H]
                vec = att_vec[:, 2 * l + n, cols].rearrange("p (a c) -> p a c", a=1).to_broadcast([P, F, HALF])
                tmp = staged[:, half].rearrange("p a d -> p (a d)").rearrange("p (k c) -> p k c", k=F)
                link(nc.vector.tensor_tensor(tmp, w, vec, ALU.mult))
                first = n * H + half * (H // 2)
                link(nc.vector.tensor_reduce(score_w[l][:, :, first:first + H // 2],
                                             tmp.rearrange("p k (h o) -> p k h o", h=H // 2), AX.X, ALU.add))

            dve.wait_ge(layer_in[0], 16 * 5)
            for n in range(2):
                for half in range(2):
                    score_weights(0, n, half)

            def read_acc(pair, phi, h, it):
                g = H * unit(pair, phi) + h
                dve.wait_ge(attended, T * g + it + 1)
                if it == 0:
                    wait(dve, combined, 6 * (g - 1))
                nc.vector.tensor_reduce(sums[h % 2][:, it],
                                        acc[it % ACCS][:, 0:2 * W3].rearrange("p (k s c) -> p k c s", k=2, s=PARTS),
                                        AX.X, ALU.add).then_inc(acc_read, 1)

            def neg_edges(pair, phi, h, c):
                g = H * unit(pair, phi) + h
                tiles = slice(c * CHUNK, (c + 1) * CHUNK)
                n32, m32 = (b[:, tiles, :].bitcast(int32) for b in (neg[h % 2], mask[phi % 2]))
                dve.wait_ge(signed, T * g + CHUNK * (c + 1))
                if phi < 2 and h == 0 and c == 0:
                    dve.wait_ge(mask_copied, T * (graph_of(pair, phi) + 1))
                nc.vector.scalar_tensor_tensor(n32, n32, SIGN_TO_EDGE, m32, ALU.logical_shift_right,
                                               ALU.bitwise_and).then_inc(neg_made, 1)

            def pos_edges(pair, phi, h, c):
                g = H * unit(pair, phi) + h
                tiles = slice(c * CHUNK, (c + 1) * CHUNK)
                n32, p32, m32 = (b[:, tiles, :].bitcast(int32) for b in (neg[h % 2], pos[h % 2], mask[phi % 2]))
                dve.wait_ge(neg_made, NCHUNK * g + c + 1)
                nc.vector.tensor_tensor(p32, n32, m32, ALU.bitwise_xor).then_inc(edges, 1)

            def rest_of_q(pair, phi, h):
                g = H * unit(pair, phi) + h
                dve.wait_ge(rounded, 2 * g + 2)
                nc.vector.tensor_tensor(y[:, 1], y[:, 1], y_parts[h % 2][:, 1, :, 0, :], ALU.subtract)\
                  .then_inc(rest, 1)

            def middle_part_v(pair, phi, h):
                dve.wait_ge(rest_v, H * unit(pair, phi) + h + 1)
                nc.vector.tensor_copy(y_parts[h % 2][:, 0, :, 1, :], y[:, 0]).then_inc(middle_v, 1)

            def low_part(pair, phi, h, k, middle):
                yp = y_parts[h % 2]
                dve.wait_ge(middle, H * unit(pair, phi) + h + 1)
                nc.vector.tensor_tensor(yp[:, k, :, 2, :], y[:, k], yp[:, k, :, 1, :], ALU.subtract).then_inc(rest, 1)

            def denominators(pair, phi, h):
                g = H * unit(pair, phi) + h
                s, r = sums[h % 2], den[h % 2]
                dve.wait_ge(combined, 6 * g + 3)
                nc.vector.tensor_scalar(r[:, 0, :], s[:, :, 0, K], 0.0, None, ALU.is_equal).then_inc(dens, 1)
                nc.vector.tensor_scalar(r[:, 1, :], s[:, :, 0, K], TINY, None, ALU.max).then_inc(dens, 1)

            def invert(pair, phi, h):
                g = H * unit(pair, phi) + h
                r = den[h % 2]
                dve.wait_ge(dens, 3 * g + 2)
                nc.vector.reciprocal(r[:, 2, :], r[:, 1, :]).then_inc(dens, 1)

            def add_residual(pair, phi, h):
                p = phi % 2
                x_h, o_h = xs[p][:, :, h * K:(h + 1) * K], o[h % 2][:, :, :]
                dve.wait_ge(combined, 6 * (H * unit(pair, phi) + h + 1))
                if phi < 2:
                    nc.vector.scalar_tensor_tensor(x_h, o_h, 0.0, x_h, ALU.max, ALU.add).then_inc(residual, 1)
                else:
                    nc.vector.tensor_tensor(x_h, o_h, x_h, ALU.add).then_inc(residual, 1)

            def norm_stats(pair, phi, t):
                if t == 0:
                    dve.wait_ge(residual, H * (unit(pair, phi) + 1))
                nc.vector.bn_stats(stats[:, t, :], xs[phi % 2][:, t, :]).then_inc(normed, 1)

            def norm_aggregate(pair, phi, t):
                dve.wait_ge(normed, 2 * (T * unit(pair, phi) + t) + 1)
                stand_apart(dve)
                nc.vector.bn_aggr(mv[:, t, :], stats[:, t, :]).then_inc(normed, 1)

            def copy_mask(g, p, it):
                dve.wait_ge(mask_ps, T * g + it + 1)
                stand_apart(dve)
                nc.vector.tensor_scalar(mask[p][:, :, it * P:(it + 1) * P], misc_b, 0.0, EDGE, ALU.is_gt, ALU.mult, saturate=False)\
                  .then_inc(mask_copied, 1)

            def guard_a(pair, phi):
                u, q = unit(pair, phi), phi % 2
                s, d = sd[q][:, :, 0:H], sd[q][:, :, H:2 * H]
                dve.wait_ge(h_copied, T * (u + 1))
                nc.vector.tensor_reduce(d_max[:, 0:H], d.rearrange("p t h -> p h t"), AX.X, ALU.max)\
                  .then_inc(guard, 1)
                bias = score_b[:, phi // 2:phi // 2 + 1, :].to_broadcast([P, T, H])
                nc.vector.tensor_tensor(s_parts[:, :, 0:H], s, bias, ALU.add)
                nc.vector.tensor_tensor(s, s, bias, ALU.add).then_inc(sT_made, 1)
                dve.wait_ge(sT_made, 4 * u + 1)
                nc.vector.tensor_tensor(s_rest[:, :, :], s, s_parts[:, :, 0:H], ALU.subtract).then_inc(sT_made, 1)
                dve.wait_ge(sT_made, 4 * u + 2)
                nc.vector.tensor_copy(s_parts[:, :, H:2 * H], s_rest[:, :, :]).then_inc(sT_made, 1)
                dve.wait_ge(sT_made, 4 * u + 3)
                nc.vector.tensor_tensor(s_parts[:, :, 2 * H:3 * H], s_rest[:, :, :], s_parts[:, :, H:2 * H],
                                        ALU.subtract).then_inc(sT_made, 1)

            def guard_b(pair, phi):
                u = unit(pair, phi)
                dve.wait_ge(guard_ps, 2 * u + 1)
                nc.vector.tensor_reduce(d_maxT[:, :], misc[:, 0:P], AX.X, ALU.max).then_inc(guard, 1)
                dve.wait_ge(guard, GUARD * u + 2)
                nc.vector.tensor_scalar(d_diag[:, :], ident[:, 0:H], d_maxT[:, 0:1], None, ALU.mult)\
                  .then_inc(guard, 1)

            def guard_c(pair, phi):
                u, q = unit(pair, phi), phi % 2
                s, d = sd[q][:, :, 0:H], sd[q][:, :, H:2 * H]
                dve.wait_ge(guard_ps, 2 * u + 2)
                nc.vector.tensor_copy(d_top[:, :], misc[:, 0:H]).then_inc(guard, 1)
                dve.wait_ge(guard, GUARD * u + 4)
                top = d_top[:, :].rearrange("p (a h) -> p a h", a=1).to_broadcast([P, T, H])
                nc.vector.tensor_tensor(args[:, 2], d, top, ALU.subtract)
                nc.vector.tensor_tensor(zt[:, :, :], s, top, ALU.add).then_inc(guard, 1)
                dve.wait_ge(guard, GUARD * u + 5)
                nc.vector.tensor_scalar(args[:, 0], zt[:, :, :], 1.0 - SLOPE, 0.0, ALU.mult, ALU.min)
                nc.vector.tensor_scalar(args[:, 1], zt[:, :, :], SLOPE - 1.0, 0.0, ALU.mult, ALU.min)
                nc.vector.tensor_scalar(args[:, 3], args[:, 2], SLOPE, None, ALU.mult).then_inc(guard, 1)

            def copy_sT(pair, phi):
                dve.wait_ge(sT_ps, unit(pair, phi) + 1)
                nc.vector.tensor_copy(sT[phi % 2][:, :].rearrange("p (t n) -> p t n", t=T), misc_b)\
                  .then_inc(sT_copied, 1)

            POS_EDGES = {1: 0, 3: 1, 4: 2, 6: 3}
            NORM = {(1, 2): 0, (1, 6): 1, (2, 2): 2, (2, 3): 3, (2, 6): 4, (3, 0): 5, (3, 2): 6, (3, 4): 7}

            def phase(pair, phi):
                attn, prep, ends = parts_of(pair, phi)
                nxt, prv = next_phase(pair, phi), prev_phase(pair, phi)
                for h in range(H):
                    ahead, behind = heads_ahead(pair, phi, h), head_behind(pair, phi, h)
                    before = head_before(pair, phi, h)
                    for it in range(T):
                        if before and it == 0:
                            add_residual(*before)
                        if behind and it == 4:
                            denominators(*behind)
                        if ahead:
                            if it == 1:
                                neg_edges(*ahead, 0)
                            if it == 2:
                                rest_of_q(*ahead)
                            if it == 3:
                                neg_edges(*ahead, 1)
                            if it == 4:
                                middle_part_v(*ahead)
                                neg_edges(*ahead, 2)
                            if it == 5:
                                low_part(*ahead, 1, middle_q)
                                low_part(*ahead, 0, middle_v)
                            if it == 6:
                                neg_edges(*ahead, 3)
                        norm = NORM.get((h, it)) if ends else None
                        if norm is not None:
                            norm_stats(*prv, norm)
                        if attn:
                            read_acc(pair, phi, h, it)
                        if norm is not None:
                            norm_aggregate(*prv, norm)
                        if behind and it == 4:
                            invert(*behind)
                        if ahead and it in POS_EDGES:
                            pos_edges(*ahead, POS_EDGES[it])
                        if isinstance(pair, int) and (pair, phi) == (0, 0) and 1 <= h <= 4 and it == 2:
                            if h == 1:
                                dve.wait_ge(layer_in[1], 16 * (2 * F + 2))
                            score_weights(1, (h - 1) // 2, (h - 1) % 2)
                        if prep and phi in (0, 3) and job(MASK_AT, h, it) is not None:
                            copy_mask(mask_graph(pair, phi), (phi + 1) % 2, job(MASK_AT, h, it))
                        if prep and (h, it) == (5, 7):
                            guard_a(*nxt)
                        if prep and h == 6:
                            if it == 1:
                                guard_b(*nxt)
                            if it == 3:
                                guard_c(*nxt)
                            if it == 5:
                                copy_sT(*nxt)

            phases(dve, phase)

        @block.tensor
        def _(pe):
            def rows_of_s(pair, phi, h):
                u, q = unit(pair, phi), phi % 2
                g = H * u + h
                if h == 0:
                    pe.wait_ge(sT_copied, u + 1)
                if isinstance(pair, int) and g == 0:
                    pe.wait_ge(select_loaded, 16)
                wait(pe, signed, T * g)
                for k in range(2):
                    last = nc.tensor.matmul(s_ps[:, k * 512:(k + 1) * 512], select[:, h, :],
                                            sT[q][:, k * 512:(k + 1) * 512], start=True, stop=True)
                last.then_inc(s_rows, 1)

            def attend(pair, phi, h, it):
                g = H * unit(pair, phi) + h
                n = T * g + it
                wait(pe, acc_read, n - ACCS + 1)
                if it == 0:
                    pe.wait_ge(rest, 3 * g + 3)
                stand_apart(pe)
                cols = slice(it * P, (it + 1) * P)
                for k, edge in enumerate((pos[h % 2], neg[h % 2])):
                    for t in range(T):
                        if it == 0 and k == 0 and t % CHUNK == 0:
                            pe.wait_ge(edges, NCHUNK * g + t // CHUNK + 1)
                            stand_apart(pe)
                        last = nc.tensor.matmul(acc[it % ACCS][:, k * W3:(k + 1) * W3], edge[:, t, cols],
                                                y_parts[h % 2][:, k, t].rearrange("p s c -> p (s c)"),
                                                start=(t == 0), stop=(t == T - 1))
                last.then_inc(attended, 1)

            def transpose_mask(g, it):
                pe.wait_ge(adj_in[it % 2], 16 * (T // 2 * g + it // 2 + 1))
                for t in range(T):
                    last = nc.tensor.transpose(misc_b[:, t, :], adj_rows[:, it % 2, t * P:(t + 1) * P], ident_b[:, :])
                last.then_inc(mask_ps, 1)

            def transpose_x(pair, phi, t):
                u, p = unit(pair, phi), phi % 2
                if phi < 2:
                    if t % PAIR == 0:
                        pe.wait_ge(x_in[p][t // PAIR], 16 * (pair + 1))
                else:
                    pe.wait_ge(applied, T * (u - 2) + t + 1)
                for k in range(F):
                    last = nc.tensor.transpose(misc[:, k * P:(k + 1) * P], xs[p][:, t, k * P:(k + 1) * P], ident[:, :])
                last.then_inc(xT_ps, 1)

            def project(pair, phi, t):
                u, l = unit(pair, phi), phi // 2
                n = T * u + t
                pe.wait_ge(xT_copied, n + 1)
                if isinstance(pair, int) and n == 0:
                    pe.wait_ge(setup_dve, 2 + 8)
                for bank, cols in ((misc, slice(HALF + 2 * H, D + 2 * H)), (wide, slice(0, HALF + 2 * H))):
                    if bank is wide and t == 0:
                        wait(pe, mean_copied, u)
                    elif bank is wide:
                        pe.wait_ge(h_copied, n)
                    for k in range(F):
                        last = nc.tensor.matmul(bank[:, 0:cols.stop - cols.start], xT[:, t % 2, k, :],
                                                weight[l][:, k, cols], start=(k == 0), stop=(k == F - 1))
                    last.then_inc(h_ps, 1)

            def phase(pair, phi):
                attn, prep, ends = parts_of(pair, phi)
                nxt = next_phase(pair, phi)
                u = unit(*nxt)
                empty = (mask_copied, T * (2 * pair + 1 + phi)) if phi < 2 else (sT_copied, u)
                for h in range(H):
                    ahead = heads_ahead(pair, phi, h)
                    for it in range(T):
                        if ahead and (h, it) == (H - 1, 0):
                            rows_of_s(*ahead)
                        if it == T - 1 and h != H - 2:
                            after = (pair, phi, h + 2) if h < H - 2 else (*nxt, 1)
                            if (attn if h < H - 2 else prep):
                                rows_of_s(*after)
                        if attn:
                            attend(pair, phi, h, it)
                        if not prep:
                            continue
                        if job(TURN_AT, h, it) is not None:
                            wait(pe, *empty)
                            transpose_x(*nxt, job(TURN_AT, h, it))
                        if job(PROJECT_AT, h, it) is not None:
                            t = job(PROJECT_AT, h, it)
                            project(*nxt, t)
                            empty = (half_copied, T * u + t + 1)
                        if h == 6 and it == 0:
                            wait(pe, *empty)
                            pe.wait_ge(guard, GUARD * u + 1)
                            nc.tensor.transpose(misc[:, 0:P], d_max[:, :], ident[:, :]).then_inc(guard_ps, 1)
                        if h == 6 and it == 2:
                            pe.wait_ge(guard, GUARD * u + 3)
                            nc.tensor.matmul(misc[:, 0:H], ones[:, :], d_diag[:, :], start=True, stop=True)\
                              .then_inc(guard_ps, 1)
                        if h == 6 and it == 4:
                            pe.wait_ge(guard, GUARD * u + 4)
                            pe.wait_ge(sT_made, 4 * (u + 1))
                            for t in range(T):
                                last = nc.tensor.transpose(misc_b[:, t, :], s_parts[:, t, :], ident_b[:, :])
                            last.then_inc(sT_ps, 1)
                            empty = (sT_copied, u + 1)
                        if phi in (0, 3) and job(MASK_AT, h, it) is not None:
                            g, t = mask_graph(pair, phi), job(MASK_AT, h, it)
                            wait(pe, *empty)
                            transpose_mask(g, t)
                            empty = (mask_copied, T * g + t + 1)
                        if h == 7 and it == 3:
                            pe.wait_ge(summed, (T - 1) * (u + 1))
                            pe.wait_ge(h_copied, T * (u + 1))
                            nc.tensor.matmul(wide[:, :], ones[:, :], h_sum[:, :], start=True, stop=True)\
                              .then_inc(mean_ps, 1)
                if isinstance(pair, int) and (pair, phi) == (0, 0):
                    pe.wait_ge(setup_dve, 2 + 16)

            pe.wait_ge(setup_dve, 2)
            phases(pe, phase)


def kernel(x, adj, L0_gnn_W_proj, L0_gnn_W_att, L0_gnn_b_att, L1_gnn_W, L1_gnn_a1, L1_gnn_a2):
    import concourse.bacc as bacc
    from concourse.bass_utils import run_bass_kernel_spmd

    nc = bacc.Bacc("TRN2", target_bir_lowering=False, num_devices=1)
    select = np.zeros((P, H, P), np.uint16)
    for part in range(PARTS):
        for h in range(H):
            select[part * H + h, h, :] = 0x3F80
    ins = {
        "x": np.ascontiguousarray(x), "adj": np.ascontiguousarray(adj), "W0": np.ascontiguousarray(L0_gnn_W_proj),
        "att0": np.ascontiguousarray(L0_gnn_W_att), "b0": np.ascontiguousarray(L0_gnn_b_att),
        "W1": np.ascontiguousarray(L1_gnn_W), "a1": np.ascontiguousarray(L1_gnn_a1),
        "a2": np.ascontiguousarray(L1_gnn_a2), "ident": np.eye(P, dtype=np.float32), "select": select,
    }
    aps = [nc.dram_tensor(f"in_{n}", a.shape, mybir.dt.from_np(a.dtype), kind="ExternalInput").ap()
           for n, a in ins.items()]
    out = nc.dram_tensor("out_x", (B, N, D), fp32, kind="ExternalOutput").ap()
    gat_two_layers(nc, *aps, out)
    r = run_bass_kernel_spmd(nc, [{f"in_{n}": a for n, a in ins.items()}], core_ids=[0])
    return r.results[0]["out_x"]
```
